# Optimizing a Trainium2 kernel written in Bass

```python
import numpy as np
import jax
import jax.numpy as jnp

def _softmax(x, axis=-1):
    return jax.nn.softmax(x, axis=axis)

def _gelu(x):
    return jax.nn.gelu(x, approximate=True)

def _silu(x):
    return jax.nn.silu(x)

def _sigmoid(x):
    return jax.nn.sigmoid(x)

def _layernorm(x, axis=-1, eps=1e-05):
    m = jnp.mean(x, axis=axis, keepdims=True)
    v = jnp.var(x, axis=axis, keepdims=True)
    return (x - m) / jnp.sqrt(v + eps)

def _scatter_add(tgt, idx, src, axis=0):
    return tgt.at[idx].add(src)

def _segment_sum(src, seg, n):
    return jax.ops.segment_sum(src, seg, n)
kernel_name = 'mk_flamingo_gated_d1_seqx_r4_794a13'

def setup_inputs(seed: int=0):
    np.random.seed(seed)
    _w = jnp.asarray

    def _rec_inputs():
        import jax
        import jax.numpy as jnp
        _rk = jax.random.key(seed)
        x = 7.22e-05 + 1 * jax.random.normal(jax.random.fold_in(_rk, 1), (2, 1024, 256), jnp.float32)
        _lenS = 1024 - jax.random.randint(jax.random.fold_in(_rk, 7), (2,), 0, max(1, 1024 // 4) + 1, jnp.int32)
        _lenS2 = 77 - jax.random.randint(jax.random.fold_in(_rk, 8), (2,), 0, max(1, 77 // 4) + 1, jnp.int32)
        _ctx_768P = jax.random.normal(jax.random.fold_in(_rk, 11), (2, 16, 192), jnp.float32)
        _ctx_768c = jax.random.dirichlet(jax.random.fold_in(_rk, 511), 0.3 * jnp.ones((16,), jnp.float32), (2, 77))
        _ctx_768t = jnp.einsum('bsk,bkd->bsd', _ctx_768c, _ctx_768P)
        _ctx_768t = _ctx_768t * jax.lax.rsqrt(jnp.mean(jnp.square(_ctx_768t)) + 1e-12) * 0.953939
        ctx_768 = -0.000191848 + 0.999787 * (_ctx_768t + 0.3 * jax.random.normal(jax.random.fold_in(_rk, 611), (2, 77, 192), jnp.float32))
        _validS = jnp.arange(1024)[None, :] < _lenS[:, None]
        _validS2 = jnp.arange(77)[None, :] < _lenS2[:, None]
        _causal = jnp.tril(jnp.ones((1024, 1024), dtype=bool))
        mask_BxS2_bk0 = jnp.logical_not(jnp.broadcast_to(_validS2[:, :], (2, 77)))
        _g = jax.random.normal(jax.random.fold_in(_rk, 9001), (2, 1), jnp.float32)
        _g = jnp.sign(_g) * jnp.maximum(jnp.abs(_g), 1.0) + (_g == 0) * 1.0
        g_xattn = _g[0]
        g_ffn = _g[1]
        return (x, ctx_768, mask_BxS2_bk0, g_xattn, g_ffn)
    x, ctx_768, mask_BxS2_bk0, g_xattn, g_ffn = _rec_inputs()

    def _L0_xattn_setup():
        import jax, jax.numpy as jnp
        import numpy as np
        HEADS = 8
        DIM_HEAD = 64
        QUERY_DIM = 256
        CONTEXT_DIM = 192
        INNER = HEADS * DIM_HEAD
        key = jax.random.key(seed)
        ks = jax.random.split(key, 8)
        b, n, j = (4, 512, 512)
        x = jax.random.normal(ks[0], (b, n, QUERY_DIM), dtype=jnp.float32)
        context = jax.random.normal(ks[1], (b, j, CONTEXT_DIM), dtype=jnp.float32)
        mask = jax.random.randint(ks[2], (b, j), 0, 2).astype(jnp.bool_)
        W_q = jax.random.normal(ks[3], (QUERY_DIM, INNER), dtype=jnp.float32) / np.sqrt(QUERY_DIM)
        W_k = jax.random.normal(ks[4], (CONTEXT_DIM, INNER), dtype=jnp.float32) / np.sqrt(CONTEXT_DIM)
        W_v = jax.random.normal(ks[5], (CONTEXT_DIM, INNER), dtype=jnp.float32) / np.sqrt(CONTEXT_DIM)
        W_o = jax.random.normal(ks[6], (INNER, QUERY_DIM), dtype=jnp.float32) / np.sqrt(INNER)
        b_o = jax.random.normal(ks[7], (QUERY_DIM,), dtype=jnp.float32) * 0.01
        return {'x': x, 'context': context, 'mask': mask, 'W_q': W_q, 'W_k': W_k, 'W_v': W_v, 'W_o': W_o, 'b_o': b_o}
    _L0_xattn_all = _L0_xattn_setup()
    _L0_xattn_in = {k: v for k, v in _L0_xattn_all.items() if k in ('W_q', 'W_k', 'W_v', 'W_o', 'b_o')}
    del _L0_xattn_all

    def _L0_ffn_setup():
        import jax, jax.numpy as jnp
        import numpy as np

        def _bitlinear(x, w_latent):
            scale = jax.lax.stop_gradient(jnp.clip(jnp.mean(jnp.abs(w_latent), axis=1, keepdims=True), 1e-05, None))
            tern = jnp.clip(jnp.round(w_latent / scale), -1.0, 1.0)
            w = w_latent + jax.lax.stop_gradient(tern - w_latent)
            return x @ (w * scale).T
        key = jax.random.key(seed)
        ks = jax.random.split(key, 6)
        dim, hidden, rank = (256, 1024, 16)
        B, S = (4, 1024)
        x = jax.random.normal(ks[0], (B, S, dim), dtype=jnp.float32)
        w_fc = 0.02 * jax.random.normal(ks[1], (hidden, dim), dtype=jnp.float32)
        w_proj = 0.02 * jax.random.normal(ks[2], (dim, hidden), dtype=jnp.float32)
        u = 0.02 * jax.random.normal(ks[3], (hidden, rank), dtype=jnp.float32)
        v = 0.02 * jax.random.normal(ks[4], (rank, dim), dtype=jnp.float32)
        fast_b = jax.random.normal(ks[5], (rank, rank), dtype=jnp.float32)
        gate = jnp.float32(0.05)
        return {'x': x, 'fast_b': fast_b, 'w_fc': w_fc, 'w_proj': w_proj, 'u': u, 'v': v, 'gate': gate}
    _L0_ffn_all = _L0_ffn_setup()
    _L0_ffn_in = {k: v for k, v in _L0_ffn_all.items() if k in ('fast_b', 'w_fc', 'w_proj', 'u', 'v', 'gate')}
    del _L0_ffn_all
    return {'x': x, 'ctx_768': ctx_768, 'mask_BxS2_bk0': mask_BxS2_bk0, 'g_xattn': g_xattn, 'g_ffn': g_ffn, 'L0_xattn_W_q': _L0_xattn_in['W_q'], 'L0_xattn_W_k': _L0_xattn_in['W_k'], 'L0_xattn_W_v': _L0_xattn_in['W_v'], 'L0_xattn_W_o': _L0_xattn_in['W_o'], 'L0_xattn_b_o': _L0_xattn_in['b_o'], 'L0_ffn_fast_b': _L0_ffn_in['fast_b'], 'L0_ffn_w_fc': _L0_ffn_in['w_fc'], 'L0_ffn_w_proj': _L0_ffn_in['w_proj'], 'L0_ffn_u': _L0_ffn_in['u'], 'L0_ffn_v': _L0_ffn_in['v'], 'L0_ffn_gate': _L0_ffn_in['gate']}

def reference(x, ctx_768, mask_BxS2_bk0, g_xattn, g_ffn, L0_xattn_W_q, L0_xattn_W_k, L0_xattn_W_v, L0_xattn_W_o, L0_xattn_b_o, L0_ffn_fast_b, L0_ffn_w_fc, L0_ffn_w_proj, L0_ffn_u, L0_ffn_v, L0_ffn_gate):
    import jax
    import jax.numpy as jnp

    def _L0_xattn_ref(x, context, mask, W_q, W_k, W_v, W_o, b_o):
        import jax, jax.numpy as jnp
        import numpy as np
        HEADS = 8
        DIM_HEAD = 64
        QUERY_DIM = 256
        CONTEXT_DIM = 192
        INNER = HEADS * DIM_HEAD
        b, n, _ = x.shape
        j = context.shape[1]
        scale = DIM_HEAD ** (-0.5)
        q = (x @ W_q).reshape(b, n, HEADS, DIM_HEAD)
        k = (context @ W_k).reshape(b, j, HEADS, DIM_HEAD)
        v = (context @ W_v).reshape(b, j, HEADS, DIM_HEAD)
        sim = jnp.einsum('bihd,bjhd->bhij', q, k) * scale
        max_neg = -jnp.finfo(sim.dtype).max
        sim = jnp.where(mask[:, None, None, :], sim, max_neg)
        attn = jax.nn.softmax(sim, axis=-1)
        out = jnp.einsum('bhij,bjhd->bihd', attn, v).reshape(b, n, INNER)
        return out @ W_o + b_o

    def _L0_ffn_ref(x, fast_b, w_fc, w_proj, u, v, gate):
        import jax, jax.numpy as jnp
        import numpy as np

        def _bitlinear(x, w_latent):
            scale = jax.lax.stop_gradient(jnp.clip(jnp.mean(jnp.abs(w_latent), axis=1, keepdims=True), 1e-05, None))
            tern = jnp.clip(jnp.round(w_latent / scale), -1.0, 1.0)
            w = w_latent + jax.lax.stop_gradient(tern - w_latent)
            return x @ (w * scale).T
        h = _bitlinear(x, w_fc) + gate * (x @ v.T @ fast_b.T @ u.T)
        r = jnp.maximum(h, 0.0)
        return _bitlinear(r * r, w_proj)
    x = x + jnp.tanh(g_xattn[0]) * _L0_xattn_ref(_layernorm(x, axis=-1), ctx_768, mask_BxS2_bk0, L0_xattn_W_q, L0_xattn_W_k, L0_xattn_W_v, L0_xattn_W_o, L0_xattn_b_o)
    x = x + jnp.tanh(g_ffn[0]) * _L0_ffn_ref(_layernorm(x, axis=-1), L0_ffn_fast_b, L0_ffn_w_fc, L0_ffn_w_proj, L0_ffn_u, L0_ffn_v, L0_ffn_gate)
    return x

_drawn_inputs = setup_inputs


def setup_inputs(seed=0):
    import zlib

    import numpy as np

    out = dict(_drawn_inputs(seed))
    spreads = {}
    factors = {'L0_xattn_b_o': 8.0, 'L0_ffn_fast_b': 8.0, 'L0_ffn_u': 8.0, 'L0_ffn_v': 8.0}
    for name, (base, spread) in spreads.items():
        noise = np.random.default_rng([zlib.crc32(name.encode()), seed]).standard_normal(out[name].shape)
        drawn = base * np.exp(spread * noise) if base else spread * noise
        out[name] = jnp.asarray(drawn.astype(out[name].dtype))
    for name, factor in factors.items():
        out[name] = (out[name] * factor).astype(out[name].dtype)
    return out
```

```python
from contextlib import ExitStack

import concourse.bass as bass
from concourse import mybir

ALU = mybir.AluOpType
ACT = mybir.ActivationFunctionType
AX = mybir.AxisListType
F32 = mybir.dt.float32
F32R = mybir.dt.float32r
BF16 = mybir.dt.bfloat16
U8 = mybir.dt.uint8

P = 128
LN_EPS = 1e-5
SCALE_FLOOR = 1e-5
MASKED = -3.38e38


def block_kernel(nc, x, context, mask, g_xattn, g_ffn, w_q, w_k, w_v, w_o, b_o, fast_b, w_fc, w_proj,
                 u, v, gate, out):
    B, SEQ, D = x.shape
    J, C = context.shape[1:]
    INNER = w_q.shape[1]
    DH = 64
    HEADS = INNER // DH
    HID = w_fc.shape[0]
    RANK = u.shape[1]
    TT = 4
    TOK = TT * P
    NS = B * SEQ // TOK
    SPB = SEQ // TOK
    KD = D // P
    KI = INNER // P
    KH = HID // P
    HJ = HEADS * J
    HALF = HJ // 2
    BJ = B * J
    KC = (HJ + P - 1) // P
    C1 = C - P
    LASTROWS = HJ - (KC - 1) * P
    ATTN_SCALE = DH ** -0.5

    ctx = ExitStack()
    with ctx:
        def sb(name, shape, dt=F32):
            return ctx.enter_context(nc.sbuf_tensor(name, shape, dt))

        def sem(name):
            return ctx.enter_context(nc.semaphore(name))

        with ExitStack() as passing:
            def early(name, shape, dt=F32):
                return passing.enter_context(nc.sbuf_tensor(name, shape, dt))

            wq_sb = early("wq_sb", [P, KD, INNER])
            wk_sb = early("wk_sb", [P, 2, INNER])
            wv_sb = early("wv_sb", [P, 2, INNER])
            wo_sb = early("wo_sb", [P, KI, D])
            wqT = early("wqT", [P, KI, D])
            kT = early("kT", [P, HEADS, BJ])
            vT = early("vT", [P, B, KI, 2 * P])
        pT_hi = sb("pT_hi", [P, KC, TOK], F32R)
        pT_lo = sb("pT_lo", [P, KC, TOK], F32R)
        x2nT_hi = sb("x2nT_hi", [P, KD, TOK], F32R)
        x2nT_lo = sb("x2nT_lo", [P, KD, TOK], F32R)
        x2n = sb("x2n", [P, TT, D])
        y_scaled = sb("y_scaled", [P, 2, D])
        with ExitStack() as passing:
            wfc_sb = early("wfc_sb", [P, KH, D])
            wproj_sb = early("wproj_sb", [P, KD, HID])
            below1 = early("below1", [P, KH, D])
            tern1 = early("tern1", [P, KH, D])
            below2 = early("below2", [P, KD, HID], BF16)
            tern2 = early("tern2", [P, KD, HID], BF16)
        r2_hi = sb("r2_hi", [P, KH, TOK], F32R)
        r2_lo = sb("r2_lo", [P, KH, TOK], F32R)
        relu = sb("relu", [P, 2, TOK])
        square = sb("square", [P, 2, TOK])
        x_sb = sb("x_sb", [P, NS, TT, D])
        ctx_sb = sb("ctx_sb", [P, 2, 2 * P])
        bo_row = sb("bo_row", [P, D])
        u_sb = sb("u_sb", [P, KH, RANK])
        v_sb = sb("v_sb", [RANK, D])
        fb_sb = sb("fb_sb", [RANK, RANK])
        gates = sb("gates", [P, 3])
        mask_row = sb("mask_row", [1, B, J], U8)
        ident = sb("ident", [P, P])
        ident_bf = sb("ident_bf", [P, P], BF16)
        ones = sb("ones", [P, P])
        ones_bf = sb("ones_bf", [P, P], BF16)
        head0_rows = sb("head0_rows", [P, P])
        minus_half = sb("minus_half", [P, TT])
        tanh_g = sb("tanh_g", [P, 2])
        ctxT = sb("ctxT", [P, 2, 2 * P])
        a_hi = sb("a_hi", [P, KD, B, HJ], F32R)
        a_lo = sb("a_lo", [P, KD, B, HJ], F32R)
        vo_hi = sb("vo_hi", [P, B * KC, D], F32R)
        vo_lo = sb("vo_lo", [P, B * KC, D], F32R)
        mask_bias = sb("mask_bias", [P, B, HJ], BF16)
        scale1 = sb("scale1", [P, KH, 3])
        scale2 = sb("scale2", [P, KD, 3])
        uT = sb("uT", [RANK, KH, P])
        fbT = sb("fbT", [RANK, RANK])
        bv = sb("bv", [RANK, D])
        w1_hi = sb("w1_hi", [P, KD, KH, P], F32R)
        w1_lo = sb("w1_lo", [P, KD, KH, P], F32R)
        w2T = sb("w2T", [P, KH, D], F32R)
        diag2 = sb("diag2", [P, KD, P])
        col_scale = sb("col_scale", [P, D])
        xn = sb("xn", [P, TT, D])
        xnT_hi = sb("xnT_hi", [P, KD, TOK], F32R)
        xnT_lo = sb("xnT_lo", [P, KD, TOK], F32R)
        stats1 = sb("stats1", [P, TT, 6])
        moments1 = sb("moments1", [P, TT, 2])
        var1 = sb("var1", [P, TT])
        rstd1 = sb("rstd1", [P, TT])
        stats2 = sb("stats2", [P, TT, 6])
        moments2 = sb("moments2", [P, TT, 2])
        var2 = sb("var2", [P, TT])
        rstd2 = sb("rstd2", [P, TT])
        neg_max = sb("neg_max", [P, TT, HEADS])
        row_sum = sb("row_sum", [P, TT, HEADS])
        inv_sum = sb("inv_sum", [P, TT, HEADS])
        probs = sb("probs", [P, TT, HJ])

        ps_s = ctx.enter_context(nc.psum_tensor("ps_s", [P, 2, 512], F32))
        ps_t = ctx.enter_context(nc.psum_tensor("ps_t", [P, 2, 512], F32))
        ps_h = ctx.enter_context(nc.psum_tensor("ps_h", [P, 2, 512], F32))
        ps_o = ctx.enter_context(nc.psum_tensor("ps_o", [P, 2, 512], F32))
        banks = [ps_s[:, 0], ps_s[:, 1], ps_t[:, 0], ps_t[:, 1], ps_h[:, 0], ps_h[:, 1], ps_o[:, 0], ps_o[:, 1]]

        x_in = [sem(f"x_in{s}") for s in range(NS)]
        ctx_in, wq_in, wk_in, wv_in, wo_in, bo_in, mask_in = map(
            sem, ("ctx_in", "wq_in", "wk_in", "wv_in", "wo_in", "bo_in", "mask_in"))
        wfc_in, wproj_in, lowrank_in, gates_in, out_stored = map(
            sem, ("wfc_in", "wproj_in", "lowrank_in", "gates_in", "out_stored"))
        ident_ready, pads_ready, consts_ready, ident_bf_ready, tanh_ready, mask_ready = map(
            sem, ("ident_ready", "pads_ready", "consts_ready", "ident_bf_ready", "tanh_ready", "mask_ready"))
        ctxT_filled, ctxT_ready, wqT_filled, wqT_ready = map(sem, ("ctxT_filled", "ctxT_ready", "wqT_filled", "wqT_ready"))
        k_filled, k_ready, v_filled, v_ready = map(sem, ("k_filled", "k_ready", "v_filled", "v_ready"))
        a_filled, a_hi_done, a_lo_done, vo_filled, vo_hi_done, vo_lo_done = map(
            sem, ("a_filled", "a_hi_done", "a_lo_done", "vo_filled", "vo_hi_done", "vo_lo_done"))
        scale1_done, scale2_done, below1_done, below2_done, tern1_done, tern2_ready, diag2_ready = map(
            sem, ("scale1_done", "scale2_done", "below1_done", "below2_done", "tern1_done", "tern2_ready",
                  "diag2_ready"))
        prep_filled, prep_by_dve, prep_by_act, w1_hi_done = map(
            sem, ("prep_filled", "prep_by_dve", "prep_by_act", "w1_hi_done"))
        ln1_stats, ln1_moments, ln1_var, ln1_rstd, xn_ready = map(
            sem, ("ln1_stats", "ln1_moments", "ln1_var", "ln1_rstd", "xn_ready"))
        ln2_stats, ln2_moments, ln2_var, ln2_rstd, x2n_ready = map(
            sem, ("ln2_stats", "ln2_moments", "ln2_var", "ln2_rstd", "x2n_ready"))
        t_filled, t_hi_done, t_lo_done = map(sem, ("t_filled", "t_hi_done", "t_lo_done"))
        s_filled, max_done, shifted, exp_done, sum_done, inv_done, p_ready = map(
            sem, ("s_filled", "max_done", "shifted", "exp_done", "sum_done", "inv_done", "p_ready"))
        o_filled, x2_done = map(sem, ("o_filled", "x2_done"))
        h_filled, relu_done, square_done, r2_hi_done, r2_lo_done = map(
            sem, ("h_filled", "relu_done", "square_done", "r2_hi_done", "r2_lo_done"))
        y_filled, y_scaled_done, y_added = map(sem, ("y_filled", "y_scaled_done", "y_added"))

        x_dram = x.rearrange("b (s p t) d -> (b s) p (t d)", p=P, t=TT)
        out_dram = out.rearrange("b (s p t) d -> (b s) p (t d)", p=P, t=TT)
        ctx_dram = context.rearrange("b j c -> (b j) c")

        PER_S = KC + 2 * KD

        def probs_fill(i, c):
            return KD + PER_S * i + c

        def ln1_fill(i, k):
            return KD + PER_S * i + KC + k

        def ln2_fill(i, k, last):
            return KD + PER_S * i + KC + k + (0 if last else KD)

        def batch(i):
            return i // SPB

        block = ctx.enter_context(nc.Block())

        @block.sync
        def _(sp):
            sp.wait_ge(pads_ready, 2)
            sp.dma_start(ctx_sb[:, 0, 0:C], ctx_dram[0:P, :]).then_inc(ctx_in, 16)
            sp.dma_start(ctx_sb[0:BJ - P, 1, 0:C], ctx_dram[P:BJ, :]).then_inc(ctx_in, 16)
            sp.dma_start(wk_sb[:, 0, :], w_k[0:P, :]).then_inc(wk_in, 16)
            sp.dma_start(wk_sb[0:C1, 1, :], w_k[P:C, :]).then_inc(wk_in, 16)
            sp.dma_start(wq_sb[:], w_q.rearrange("(k p) n -> p k n", p=P)).then_inc(wq_in, 16)
            sp.dma_start(bo_row[0:1, :], b_o.rearrange("(a d) -> a d", a=1)).then_inc(bo_in, 16)
            sp.dma_start(wv_sb[:, 0, :], w_v[0:P, :]).then_inc(wv_in, 16)
            sp.dma_start(wv_sb[0:C1, 1, :], w_v[P:C, :]).then_inc(wv_in, 16)
            sp.dma_start(wo_sb[:], w_o.rearrange("(k p) n -> p k n", p=P)).then_inc(wo_in, 16)
            sp.dma_start(wproj_sb[:], w_proj.rearrange("(k p) n -> p k n", p=P)).then_inc(wproj_in, 16)
            for s in range(2, NS):
                sp.dma_start(x_sb[:, s].rearrange("p t d -> p (t d)"), x_dram[s]).then_inc(x_in[s], 16)

            def store(s):
                sp.wait_ge(y_added, TT * s + TT)
                sp.dma_start(out_dram[s], x_sb[:, s].rearrange("p t d -> p (t d)")).then_inc(out_stored, 16)

            with sp.Fori(0, NS) as s:
                store(s)
            sp.wait_ge(out_stored, 16 * NS)

        @block.gpsimd
        def _(pool):
            pool.memset(ctx_sb[:], 0.0).then_inc(pads_ready, 1)
            pool.memset(bo_row[:], 0.0).then_inc(pads_ready, 1)
            pool.memset(ident[:], 0.0).then_inc(consts_ready, 1)
            pool.wait_ge(consts_ready, 1)
            pool.affine_select(out=ident[:], in_=ident[:], compare_op=ALU.not_equal, fill=1.0, base=0,
                               pattern=[[-1, P]], channel_multiplier=1).then_inc(ident_ready, 1)
            pool.memset(minus_half[:], -0.5).then_inc(consts_ready, 1)
            pool.memset(kT[:], 0.0).then_inc(consts_ready, 1)
            pool.memset(mask_bias[:], 0.0).then_inc(consts_ready, 1)
            pool.memset(ones_bf[:], 1.0).then_inc(consts_ready, 1)
            pool.memset(head0_rows[:], 0.0).then_inc(consts_ready, 1)
            pool.wait_ge(consts_ready, 6)
            pool.memset(head0_rows[0:1, 0:J], 1.0).then_inc(consts_ready, 1)
            pool.memset(vT[:], 0.0).then_inc(consts_ready, 1)
            pool.memset(ones[:], 1.0).then_inc(consts_ready, 1)

            def rstd1_step(i):
                pool.wait_ge(ln1_var, i + 1)
                pool.tensor_tensor(rstd1[:], var1[:], minus_half[:], ALU.pow).then_inc(ln1_rstd, 1)

            def rstd2_step(i, half):
                pool.wait_ge(ln2_var, 2 * i + half + 1)
                pool.tensor_tensor(rstd2[:, 2 * half:2 * half + 2], var2[:, 2 * half:2 * half + 2],
                                   minus_half[:, 0:2], ALU.pow).then_inc(ln2_rstd, 1)

            def normalise(i, t):
                pool.wait_ge(inv_done, TT * i + t + 1)
                p3 = probs[:, t].rearrange("p (h j) -> p h j", h=HEADS)
                pool.tensor_tensor(p3, p3, inv_sum[:, t].unsqueeze(2).to_broadcast([P, HEADS, J]),
                                   ALU.mult).then_inc(p_ready, 1)

            def square_step(f, m, head=False):
                pool.wait_ge(relu_done, KH * f + m + 1)
                if not (head and m < 2):
                    pool.wait_ge(r2_lo_done, KH * f + m - 1)
                pool.tensor_tensor(square[:, m % 2], relu[:, m % 2], relu[:, m % 2],
                                   ALU.mult).then_inc(square_done, 1)

            def add_step(f, t):
                pool.wait_ge(y_scaled_done, TT * f + t + 1)
                pool.tensor_tensor(x_sb[:, f, t], y_scaled[:, t % 2], x_sb[:, f, t], ALU.add).then_inc(y_added, 1)

            def body(i, ffn, attn=True, last=False, head=False):
                for t in range(TT):
                    if attn:
                        normalise(i, t)
                    if ffn:
                        square_step(i - 1, t, head)
                if ffn:
                    for m in range(TT, KH):
                        square_step(i - 1, m, head)
                if attn and not last:
                    rstd1_step(i + 1)
                for t in range(TT):
                    if attn and t % 2 == 1:
                        rstd2_step(i, t // 2)
                    if ffn:
                        add_step(i - 1, t)

            rstd1_step(0)
            pool.wait_ge(scale1_done, 3)
            for t in range(KH):
                pool.tensor_scalar(below1[:, t], wfc_sb[:, t], scale1[:, t, 2:3], None,
                                   ALU.is_lt).then_inc(below1_done, 1)
            pool.wait_ge(scale2_done, 3)
            for k in range(KD):
                pool.tensor_scalar(below2[:, k], wproj_sb[:, k], scale2[:, k, 2:3], None,
                                   ALU.is_lt).then_inc(below2_done, 1)
            body(0, ffn=False)
            body(1, ffn=True, head=True)
            with pool.Fori(2, NS - 1) as i:
                body(i, ffn=True)
            body(NS - 1, ffn=True, last=True)
            body(NS, ffn=True, attn=False)

        @block.scalar
        def _(act):
            for s in range(2):
                act.dma_start(x_sb[:, s].rearrange("p t d -> p (t d)"), x_dram[s]).then_inc(x_in[s], 16)
            act.dma_start(mask_row[:], mask.rearrange("(a b) j -> a b j", a=1)).then_inc(mask_in, 16)
            for n, g in enumerate((g_xattn, g_ffn, gate)):
                act.dma_start(gates[:, n:n + 1],
                              g.rearrange("(a b) -> a b", a=1).to_broadcast([P, 1])).then_inc(gates_in, 16)
            act.dma_start(wfc_sb[:], w_fc.rearrange("(p t) d -> p t d", t=KH)).then_inc(wfc_in, 16)
            act.dma_start(u_sb[:], u.rearrange("(p t) r -> p t r", t=KH)).then_inc(lowrank_in, 16)
            act.dma_start(v_sb[:], v).then_inc(lowrank_in, 16)
            act.dma_start(fb_sb[:], fast_b).then_inc(lowrank_in, 16)

            act.wait_ge(gates_in, 48)
            act.activation(tanh_g[:], gates[:, 0:2], ACT.Tanh).then_inc(tanh_ready, 1)
            act.wait_ge(ctxT_filled, 1)
            act.activation(ctxT[:], banks[0].rearrange("p (k n) -> p k n", k=2), ACT.Identity).then_inc(ctxT_ready, 1)
            act.wait_ge(consts_ready, 3)
            for n in range(2):
                act.wait_ge(k_filled, n + 1)
                ps = banks[3 + n].rearrange("p (c n) -> p c n", c=2)[:, :, 0:BJ]
                to = kT[:, 4 * n:4 * n + 4].rearrange("p (c e) n -> p c e n", e=2)
                for e in range(2):
                    rows = slice(DH * e, DH * e + DH)
                    last = act.activation(to[rows, :, e], ps[rows], ACT.Identity, scale=ATTN_SCALE)
                last.then_inc(k_ready, 1)
            for n in range(KD * KI):
                m, c = divmod(n, KI)
                act.wait_ge(a_filled, n + 1)
                act.activation(a_hi[:, m, :, 2 * c * J:2 * (c + 1) * J].rearrange("p b (h j) -> p h b j", h=2),
                               banks[(5 + n) % 8][:, 0:2 * BJ].rearrange("p (h b j) -> p h b j", h=2, b=B),
                               ACT.Identity).then_inc(a_hi_done, 1)

            def split_hi(f, k, to):
                act.wait_ge(t_filled, f + 1)
                act.activation(to, k, ACT.Identity).then_inc(t_hi_done, 1)

            def exp_step(i, t):
                act.wait_ge(shifted, TT * i + t + 1)
                act.activation(probs[:, t], probs[:, t], ACT.Exp).then_inc(exp_done, 1)

            def relu_step(f, m, head=False):
                act.wait_ge(h_filled, KH * f + m + 1)
                if not (head and m < 2):
                    act.wait_ge(square_done, KH * f + m - 1)
                act.activation(relu[:, m % 2], ps_h[:, m % 2], ACT.Relu).then_inc(relu_done, 1)
                act.wait_ge(relu_done, KH * f + m + 1)
                act.activation(r2_hi[:, m], relu[:, m % 2], ACT.Square).then_inc(r2_hi_done, 1)

            def body(i, ffn, attn=True, last=False, head=False):
                for t in range(TT):
                    if attn:
                        exp_step(i, t)
                    if ffn:
                        relu_step(i - 1, t, head)
                ffn_tiles = list(range(TT, KH)) if ffn else []
                for m in ffn_tiles[:2]:
                    relu_step(i - 1, m)
                for c in range(KC if attn else 0):
                    split_hi(probs_fill(i, c), ps_t[:, c % 2], pT_hi[:, c])
                    if c % 2 == 1 and ffn:
                        relu_step(i - 1, ffn_tiles[2 + c // 2])
                if not attn:
                    for m in ffn_tiles[2:]:
                        relu_step(i - 1, m)
                if attn and not last:
                    for k in range(KD):
                        split_hi(ln1_fill(i, k), ps_t[:, (1 + k) % 2], xnT_hi[:, k])
                if attn:
                    for k in range(KD):
                        split_hi(ln2_fill(i, k, last), ps_t[:, (1 + k) % 2], x2nT_hi[:, k])

            for k in range(KD):
                split_hi(k, ps_t[:, (1 + k) % 2], xnT_hi[:, k])
            for n in range(B * KC // 2):
                act.wait_ge(vo_filled, n + 1)
                act.activation(vo_hi[:, 2 * n:2 * n + 2], banks[(7, 4, 5, 6, 7)[n]].rearrange("p (k d) -> p k d", k=2),
                               ACT.Identity, scale=tanh_g[:, 0:1]).then_inc(vo_hi_done, 1)
            for n in range(KD * KH // 4):
                act.wait_ge(prep_filled, 9 + n)
                act.activation(w1_hi[:, n // 2, 4 * (n % 2):4 * (n % 2) + 4],
                               ps_h[:, n % 2].rearrange("p (t n) -> p t n", t=4), ACT.Identity).then_inc(w1_hi_done, 1)
            for n in range(2):
                act.wait_ge(prep_filled, 13 + n)
                act.activation(w2T[:, 4 * n:4 * n + 4], ps_h[:, n].bitcast(BF16).rearrange("p (t d) -> p t d", t=4),
                               ACT.Identity).then_inc(prep_by_act, 1)
            body(0, ffn=False)
            body(1, ffn=True, head=True)
            with act.Fori(2, NS - 1) as i:
                body(i, ffn=True)
            body(NS - 1, ffn=True, last=True)
            body(NS, ffn=True, attn=False)

        @block.vector
        def _(dve):
            def settled():
                dve.wait_ge(ident_ready, 1)

            def ln1_stats_step(i, t):
                settled()
                dve.bn_stats(stats1[:, t], x_sb[:, i, t]).then_inc(ln1_stats, 1)

            def ln1_moments_step(i):
                dve.wait_ge(ln1_stats, TT * i + TT)
                settled()
                for t in range(TT):
                    last = dve.bn_aggr(moments1[:, t], stats1[:, t])
                last.then_inc(ln1_moments, 1)
                dve.wait_ge(ln1_moments, i + 1)
                dve.tensor_scalar(var1[:], moments1[:, :, 1], LN_EPS, None, ALU.add).then_inc(ln1_var, 1)

            def ln1_normalise(i):
                dve.wait_ge(ln1_rstd, i + 1)
                for t in range(TT):
                    last = dve.tensor_scalar(xn[:, t], x_sb[:, i, t], moments1[:, t, 0:1], rstd1[:, t:t + 1],
                                             ALU.subtract, ALU.mult)
                last.then_inc(xn_ready, 1)

            def residual(i, t):
                dve.wait_ge(o_filled, TT * i + t + 1)
                dve.tensor_tensor(x_sb[:, i, t], ps_o[:, 0, 0:D], x_sb[:, i, t], ALU.add).then_inc(x2_done, 1)
                dve.wait_ge(x2_done, TT * i + t + 1)
                settled()
                dve.bn_stats(stats2[:, t], x_sb[:, i, t]).then_inc(ln2_stats, 1)
                dve.wait_ge(ln2_stats, TT * i + t + 1)
                settled()
                dve.bn_aggr(moments2[:, t], stats2[:, t]).then_inc(ln2_moments, 1)

            def ln2_var_step(i, half):
                dve.wait_ge(ln2_moments, TT * i + 2 * half + 2)
                dve.tensor_scalar(var2[:, 2 * half:2 * half + 2], moments2[:, 2 * half:2 * half + 2, 1], LN_EPS,
                                  None, ALU.add).then_inc(ln2_var, 1)

            def ln2_normalise(i, half):
                dve.wait_ge(ln2_rstd, 2 * i + half + 1)
                for t in (2 * half, 2 * half + 1):
                    last = dve.tensor_scalar(x2n[:, t], x_sb[:, i, t], moments2[:, t, 0:1], rstd2[:, t:t + 1],
                                             ALU.subtract, ALU.mult)
                last.then_inc(x2n_ready, 1)

            def split_lo(f, ps, hi, lo):
                dve.wait_ge(t_hi_done, f + 1)
                dve.tensor_tensor(lo, ps, hi.bitcast(F32), ALU.subtract).then_inc(t_lo_done, 1)

            heads4 = ps_s[:, :, 0:HALF].rearrange("p b (h j) -> p b h j", h=HEADS // 2)

            def shift_step(i, t):
                dve.wait_ge(s_filled, TT * i + t + 1)
                dve.tensor_reduce(neg_max[:, t], heads4, AX.X, ALU.max, negate=True).then_inc(max_done, 1)
                dve.wait_ge(max_done, TT * i + t + 1)
                shift = neg_max[:, t].rearrange("p (b h) -> p b h", b=2).unsqueeze(3).to_broadcast([P, 2, HEADS // 2, J])
                dve.tensor_tensor(probs[:, t].rearrange("p (b h j) -> p b h j", b=2, h=HEADS // 2), heads4, shift,
                                  ALU.add).then_inc(shifted, 1)

            def sum_step(i, t):
                dve.wait_ge(exp_done, TT * i + t + 1)
                dve.tensor_reduce(row_sum[:, t], probs[:, t].rearrange("p (h j) -> p h j", h=HEADS), AX.X,
                                  ALU.add).then_inc(sum_done, 1)
                dve.wait_ge(sum_done, TT * i + t + 1)
                dve.reciprocal(inv_sum[:, t], row_sum[:, t]).then_inc(inv_done, 1)

            def split_square(f, m):
                dve.wait_ge(square_done, KH * f + m + 1)
                dve.wait_ge(r2_hi_done, KH * f + m + 1)
                dve.tensor_tensor(r2_lo[:, m], square[:, m % 2], r2_hi[:, m].bitcast(F32),
                                  ALU.subtract).then_inc(r2_lo_done, 1)

            def y_step(f, t, head=False):
                dve.wait_ge(y_filled, TT * f + t + 1)
                if not (head and t < 2):
                    dve.wait_ge(y_added, TT * f + t - 1)
                dve.tensor_tensor(y_scaled[:, t % 2], ps_o[:, 1, 0:D], col_scale[:], ALU.mult).then_inc(y_scaled_done, 1)

            def body(i, ffn, attn=True, last=False, head=False):
                ahead = attn and not last
                for t in range(TT):
                    if attn:
                        shift_step(i, t)
                        if t > 0:
                            sum_step(i, t - 1)
                    if ffn and t > 0:
                        split_square(i - 1, t - 1)
                    if ahead:
                        ln1_stats_step(i + 1, t)
                if attn:
                    sum_step(i, TT - 1)
                if ahead:
                    ln1_moments_step(i + 1)
                split = list(range(TT - 1, KH)) if ffn else []
                for m in split[:3]:
                    split_square(i - 1, m)
                for c in range(KC if attn else 0):
                    split_lo(probs_fill(i, c), ps_t[:, c % 2], pT_hi[:, c], pT_lo[:, c])
                    if c % 2 == 1 and ffn:
                        split_square(i - 1, split[3 + c // 2])
                if not attn:
                    for m in split[3:]:
                        split_square(i - 1, m)
                if ahead:
                    ln1_normalise(i + 1)
                for t in range(TT - 1):
                    if attn:
                        residual(i, t)
                        if t == 1:
                            ln2_var_step(i, 0)
                        if t == 2:
                            ln2_normalise(i, 0)
                    if ffn:
                        y_step(i - 1, t, head)
                if attn:
                    residual(i, TT - 1)
                    ln2_var_step(i, 1)
                for k in range(KD):
                    if ahead:
                        split_lo(ln1_fill(i, k), ps_t[:, (1 + k) % 2], xnT_hi[:, k], xnT_lo[:, k])
                    if attn and k == 0:
                        ln2_normalise(i, 1)
                if ffn:
                    y_step(i - 1, TT - 1, head)
                if attn:
                    for k in range(KD):
                        split_lo(ln2_fill(i, k, last), ps_t[:, (1 + k) % 2], x2nT_hi[:, k], x2nT_lo[:, k])

            dve.wait_ge(x_in[0], 16)
            for t in range(TT):
                ln1_stats_step(0, t)
            ln1_moments_step(0)
            for n in range(2):
                dve.wait_ge(wqT_filled, n + 1)
                dve.tensor_copy(wqT[:, 2 * n:2 * n + 2], banks[1 + n].rearrange("p (c d) -> p c d", c=2)).then_inc(wqT_ready, 1)
            ln1_normalise(0)
            dve.wait_ge(mask_in, 16)
            dve.wait_ge(consts_ready, 4)
            for h in range(HEADS):
                last = dve.tensor_scalar(mask_bias[0:1, :, h * J:(h + 1) * J], mask_row[:], -1.0, -MASKED,
                                         ALU.add, ALU.mult)
            last.then_inc(mask_ready, 1)
            for n in range(KD * KI):
                m, c = divmod(n, KI)
                dve.wait_ge(a_hi_done, n + 1)
                view = [a[:, m, :, 2 * c * J:2 * (c + 1) * J].rearrange("p b (h j) -> p h b j", h=2) for a in (a_lo, a_hi)]
                dve.tensor_tensor(view[0], banks[(5 + n) % 8][:, 0:2 * BJ].rearrange("p (h b j) -> p h b j", h=2, b=B),
                                  view[1].bitcast(F32), ALU.subtract).then_inc(a_lo_done, 1)
            for k in range(KD):
                split_lo(k, ps_t[:, (1 + k) % 2], xnT_hi[:, k], xnT_lo[:, k])
            dve.wait_ge(consts_ready, 8)
            for n in range(2):
                dve.wait_ge(v_filled, n + 1)
                for c in (2 * n, 2 * n + 1):
                    for e in range(2):
                        rows, at = slice(DH * e, DH * e + DH), (2 * c + e) * J - P * c
                        last = dve.tensor_copy(vT[rows, :, c, at:at + J],
                                               banks[5 + n][rows, 256 * (c % 2):256 * (c % 2) + BJ].rearrange("p (b j) -> p b j", b=B))
                last.then_inc(v_ready, 1)
            dve.wait_ge(tanh_ready, 1)
            for n in range(B * KC // 2):
                dve.wait_ge(vo_hi_done, n + 1)
                dve.scalar_tensor_tensor(out=vo_lo[:, 2 * n:2 * n + 2],
                                         in0=banks[(7, 4, 5, 6, 7)[n]].rearrange("p (k d) -> p k d", k=2),
                                         scalar=tanh_g[:, 0:1], in1=vo_hi[:, 2 * n:2 * n + 2].bitcast(F32),
                                         op0=ALU.mult, op1=ALU.subtract).then_inc(vo_lo_done, 1)

            def row_scales(scales, w, done, n):
                dve.tensor_reduce(scales[:, :, 0], w, AX.X, ALU.add, apply_absolute_value=True).then_inc(done, 1)
                dve.wait_ge(done, 1)
                dve.tensor_scalar(scales[:, :, 0], scales[:, :, 0], 1.0 / n, SCALE_FLOOR, ALU.mult, ALU.max).then_inc(done, 1)
                dve.wait_ge(done, 2)
                dve.tensor_scalar(scales[:, :, 1], scales[:, :, 0], 0.5, None, ALU.mult)
                dve.tensor_scalar(scales[:, :, 2], scales[:, :, 0], -0.5, None, ALU.mult).then_inc(done, 1)

            dve.wait_ge(wfc_in, 16)
            row_scales(scale1, wfc_sb[:], scale1_done, D)
            dve.wait_ge(wproj_in, 16)
            row_scales(scale2, wproj_sb[:], scale2_done, HID)
            dve.tensor_copy(ident_bf[:], ident[:]).then_inc(ident_bf_ready, 1)
            dve.wait_ge(gates_in, 48)
            for n in range(2):
                dve.wait_ge(prep_filled, n + 1)
                dve.tensor_scalar(uT[:, 4 * n:4 * n + 4], ps_h[0:RANK, n].rearrange("r (t p) -> r t p", t=4),
                                  gates[0:RANK, 2:3], None, ALU.mult).then_inc(prep_by_dve, 1)
            dve.wait_ge(prep_filled, 3)
            dve.tensor_copy(fbT[:], ps_h[0:RANK, 0, 0:RANK]).then_inc(prep_by_dve, 1)
            dve.wait_ge(prep_filled, 4)
            dve.tensor_copy(bv[:], ps_h[0:RANK, 1, 0:D]).then_inc(prep_by_dve, 1)
            dve.wait_ge(scale1_done, 3)
            for t in range(KH):
                dve.wait_ge(below1_done, t + 1)
                dve.scalar_tensor_tensor(out=tern1[:, t], in0=wfc_sb[:, t], scalar=scale1[:, t, 1:2], in1=below1[:, t],
                                         op0=ALU.is_gt, op1=ALU.subtract).then_inc(tern1_done, 1)
            for n in range(4):
                dve.wait_ge(prep_filled, 5 + n)
                for t in (2 * n, 2 * n + 1):
                    dve.wait_ge(tern1_done, t + 1)
                    last = dve.scalar_tensor_tensor(out=wfc_sb[:, t], in0=tern1[:, t], scalar=scale1[:, t, 0:1],
                                                    in1=ps_h[:, n % 2, D * (t % 2):D * (t % 2) + D],
                                                    op0=ALU.mult, op1=ALU.add)
                last.then_inc(prep_by_dve, 1)
            dve.wait_ge(scale2_done, 3)
            for k in range(KD):
                dve.wait_ge(below2_done, k + 1)
                dve.scalar_tensor_tensor(out=tern2[:, k], in0=wproj_sb[:, k], scalar=scale2[:, k, 1:2], in1=below2[:, k],
                                         op0=ALU.is_gt, op1=ALU.subtract).then_inc(tern2_ready, 1)
            for k in range(KD):
                last = dve.tensor_scalar(diag2[:, k], ident[:], scale2[:, k, 0:1], tanh_g[:, 1:2], ALU.mult, ALU.mult)
            last.then_inc(diag2_ready, 1)
            for n in range(KD * KH // 4):
                dve.wait_ge(w1_hi_done, n + 1)
                to = [w[:, n // 2, 4 * (n % 2):4 * (n % 2) + 4] for w in (w1_lo, w1_hi)]
                dve.tensor_tensor(to[0], ps_h[:, n % 2].rearrange("p (t n) -> p t n", t=4), to[1].bitcast(F32),
                                  ALU.subtract).then_inc(prep_by_dve, 1)
            dve.wait_ge(prep_filled, 15)
            dve.tensor_copy(col_scale[:], ps_h[:, 0, 0:D]).then_inc(prep_by_dve, 1)
            for s in range(1, NS):
                dve.wait_ge(x_in[s], 16)
            body(0, ffn=False)
            body(1, ffn=True, head=True)
            with dve.Fori(2, NS - 1) as i:
                body(i, ffn=True)
            body(NS - 1, ffn=True, last=True)
            body(NS, ffn=True, attn=False)

        @block.tensor
        def _(pe):
            pe.wait_ge(ident_ready, 1)
            pe.wait_ge(ctx_in, 32)
            for k in range(2):
                for r in range(2):
                    last = pe.transpose(banks[0][:, 256 * k + P * r:256 * k + P * r + P],
                                        ctx_sb[:, r, P * k:P * k + P], ident[:])
            last.then_inc(ctxT_filled, 1)
            pe.wait_ge(wq_in, 16)
            for n in range(2):
                for c in range(2):
                    for k in range(KD):
                        cc = 2 * n + c
                        last = pe.transpose(banks[1 + n][:, 256 * c + P * k:256 * c + P * k + P],
                                            wq_sb[:, k, P * cc:P * cc + P], ident[:])
                last.then_inc(wqT_filled, 1)

            def project_context(bank, w, c):
                pe.matmul(bank[:, 0:BJ], w[:, 0, P * c:P * c + P], ctxT[:, 0, 0:BJ], start=True, stop=False)
                return pe.matmul(bank[:, 0:BJ], w[0:C1, 1, P * c:P * c + P], ctxT[0:C1, 1, 0:BJ],
                                 start=False, stop=True)

            pe.wait_ge(ctxT_ready, 1)
            pe.wait_ge(wk_in, 32)
            for n in range(2):
                for c in range(2):
                    last = project_context(banks[3 + n][:, 256 * c:256 * c + 256], wk_sb, 2 * n + c)
                last.then_inc(k_filled, 1)
            pe.wait_ge(wqT_ready, 2)
            for n in range(KD * KI):
                m, c = divmod(n, KI)
                pe.wait_ge(k_ready, c // 2 + 1)
                pe.matmul(banks[(5 + n) % 8][:, 0:2 * BJ], wqT[:, c, P * m:P * m + P], kT[:, 2 * c:2 * c + 2, :],
                          start=True, stop=True).then_inc(a_filled, 1)

            def free_t(f, j):
                if j is not None:
                    pe.wait_ge(t_lo_done, f - {0: 0, 1: 2}.get(j, 1))

            def transpose_ln(src, f, k, j=2):
                free_t(f, j)
                for t in range(TT):
                    last = pe.transpose(ps_t[:, (1 + k) % 2, P * t:P * t + P], src[:, t, P * k:P * k + P], ident[:])
                last.then_inc(t_filled, 1)

            def transpose_probs(i, c):
                if c == 0:
                    pe.wait_ge(p_ready, TT * i + TT)
                free_t(probs_fill(i, c), c)
                rows = P if c < KC - 1 else LASTROWS
                for t in range(TT):
                    last = pe.transpose(ps_t[0:rows, c % 2, P * t:P * t + P], probs[:, t, P * c:P * c + rows], ident[:])
                last.then_inc(t_filled, 1)

            def scores(i, t, first=False):
                if not first:
                    pe.wait_ge(shifted, TT * i + t)
                for half in range(2):
                    cols = slice(HALF * half, HALF * half + HALF)
                    ps = ps_s[:, half, 0:HALF]
                    pe.matmul(ps, ones_bf[:], mask_bias[:, batch(i), cols], start=True, stop=False)
                    for k in range(KD):
                        hi, lo = xnT_hi[:, k, P * t:P * t + P], xnT_lo[:, k, P * t:P * t + P]
                        pe.matmul(ps, hi, a_hi[:, k, batch(i), cols], start=False, stop=False)
                        pe.matmul(ps, hi, a_lo[:, k, batch(i), cols], start=False, stop=False)
                        last = pe.matmul(ps, lo, a_hi[:, k, batch(i), cols], start=False, stop=(k == KD - 1))
                last.then_inc(s_filled, 1)

            def attend(i, t, first=False):
                if not first:
                    pe.wait_ge(x2_done, TT * i + t)
                for c in range(KC):
                    rows = P if c < KC - 1 else LASTROWS
                    hi, lo = pT_hi[0:rows, c, P * t:P * t + P], pT_lo[0:rows, c, P * t:P * t + P]
                    at = batch(i) * KC + c
                    pe.matmul(ps_o[:, 0, 0:D], hi, vo_hi[0:rows, at], start=(c == 0), stop=False)
                    pe.matmul(ps_o[:, 0, 0:D], hi, vo_lo[0:rows, at], start=False, stop=False)
                    last = pe.matmul(ps_o[:, 0, 0:D], lo, vo_hi[0:rows, at], start=False, stop=(c == KC - 1))
                last.then_inc(o_filled, 1)

            def hidden(f, m, head=False):
                if not (head and m < 2):
                    pe.wait_ge(relu_done, KH * f + m - 1)
                ps = ps_h[:, m % 2]
                for k in range(KD):
                    pe.matmul(ps, w1_hi[:, k, m], x2nT_hi[:, k], start=(k == 0), stop=False)
                    pe.matmul(ps, w1_hi[:, k, m], x2nT_lo[:, k], start=False, stop=False)
                    last = pe.matmul(ps, w1_lo[:, k, m], x2nT_hi[:, k], start=False, stop=(k == KD - 1))
                last.then_inc(h_filled, 1)

            def project_out(f, t, first=False):
                if t == 0:
                    pe.wait_ge(r2_lo_done, KH * f + KH)
                if not (first and t == 0):
                    pe.wait_ge(y_scaled_done, TT * f + t)
                for m in range(KH):
                    pe.matmul(ps_o[:, 1, 0:D], r2_hi[:, m, P * t:P * t + P], w2T[:, m], start=(m == 0), stop=False)
                    last = pe.matmul(ps_o[:, 1, 0:D], r2_lo[:, m, P * t:P * t + P], w2T[:, m],
                                     start=False, stop=(m == KH - 1))
                last.then_inc(y_filled, 1)

            def body(i, ffn, attn=True, last=False, head=False, first=False, skip_s0=False):
                if ffn:
                    pass
                for t in range(TT):
                    if attn and not (t == 0 and skip_s0):
                        scores(i, t)
                    if ffn:
                        if t == 0:
                            pe.wait_ge(t_lo_done, (ln2_fill(i - 1, KD - 1, not attn)) + 1)
                        hidden(i - 1, t, head)
                rest = list(range(TT, KH)) if ffn else []
                for m in rest[:2]:
                    hidden(i - 1, m)
                for c in range(KC if attn else 0):
                    transpose_probs(i, c)
                    if c % 2 == 1 and ffn:
                        hidden(i - 1, rest[2 + c // 2])
                if not attn:
                    for m in rest[2:]:
                        hidden(i - 1, m)
                if attn:
                    pe.wait_ge(t_lo_done, probs_fill(i, KC - 1) + 1)
                for t in range(TT - 1):
                    if attn:
                        attend(i, t, first and t == 0)
                    if ffn:
                        project_out(i - 1, t, head)
                if attn:
                    attend(i, TT - 1)
                if attn and not last:
                    pe.wait_ge(xn_ready, i + 2)
                    for k in range(KD):
                        transpose_ln(xn, ln1_fill(i, k), k)
                if ffn:
                    project_out(i - 1, TT - 1)
                if attn:
                    pe.wait_ge(x2n_ready, 2 * i + 2)
                    for k in range(KD):
                        transpose_ln(x2n, ln2_fill(i, k, last), k)
                    if not last:
                        pe.wait_ge(t_lo_done, ln1_fill(i, KD - 1) + 1)

            pe.wait_ge(a_lo_done, KD * KI)
            pe.wait_ge(xn_ready, 1)
            for k in range(KD):
                transpose_ln(xn, k, k, j=None)
            pe.wait_ge(wv_in, 32)
            for n in range(2):
                for c in range(2):
                    last = project_context(banks[5 + n][:, 256 * c:256 * c + 256], wv_sb, 2 * n + c)
                last.then_inc(v_filled, 1)
            pe.wait_ge(t_lo_done, KD)
            pe.wait_ge(mask_ready, 1)
            scores(0, 0, first=True)
            pe.wait_ge(v_ready, 2)
            pe.wait_ge(wo_in, 16)
            pe.wait_ge(bo_in, 16)
            for n in range(B * KC // 2):
                if n == 4:
                    pe.wait_ge(vo_lo_done, 1)
                for q in range(2):
                    b, tile = divmod(2 * n + q, KC)
                    ps = banks[(7, 4, 5, 6, 7)[n]][:, D * q:D * q + D]
                    terms = [(vT[:, b, c, P * (tile - c):P * (tile - c) + P], wo_sb[:, c]) for c in (tile - 1, tile)
                             if 0 <= c < KI]
                    if tile == 0:
                        terms.append((head0_rows[:], bo_row[:]))
                    for at, (lhsT, rhs) in enumerate(terms):
                        last = pe.matmul(ps, lhsT, rhs, start=(at == 0), stop=(at == len(terms) - 1))
                last.then_inc(vo_filled, 1)
            pe.wait_ge(lowrank_in, 48)
            for n in range(2):
                pe.wait_ge(vo_lo_done, 2 + n)
                for t in range(4):
                    last = pe.matmul(ps_h[0:RANK, n, P * t:P * t + P], u_sb[:, 4 * n + t], ident[:], start=True, stop=True)
                last.then_inc(prep_filled, 1)
            pe.wait_ge(prep_by_dve, 1)
            pe.matmul(ps_h[0:RANK, 0, 0:RANK], fb_sb[:], ident[0:RANK, 0:RANK], start=True, stop=True).then_inc(prep_filled, 1)
            pe.wait_ge(prep_by_dve, 3)
            pe.matmul(ps_h[0:RANK, 1, 0:D], fbT[:], v_sb[:], start=True, stop=True).then_inc(prep_filled, 1)
            for n in range(4):
                pe.wait_ge(prep_by_dve, 4 + max(0, n - 1))
                for q in range(2):
                    last = pe.matmul(ps_h[:, n % 2, D * q:D * q + D], uT[:, 2 * n + q], bv[:], start=True, stop=True)
                last.then_inc(prep_filled, 1)
            for n in range(KD * KH // 4):
                pe.wait_ge(prep_by_dve, 8 + max(0, n - 1))
                for q in range(4):
                    last = pe.transpose(ps_h[:, n % 2, P * q:P * q + P],
                                        wfc_sb[:, 4 * (n % 2) + q, P * (n // 2):P * (n // 2) + P], ident[:])
                last.then_inc(prep_filled, 1)
            pe.wait_ge(tern2_ready, KD)
            pe.wait_ge(ident_bf_ready, 1)
            t2 = tern2[:].rearrange("p k (q t) -> p k t q", t=KH)
            for n in range(2):
                pe.wait_ge(prep_by_dve, 11 + n)
                ps = ps_h[:, n].bitcast(BF16).rearrange("p (t d) -> p t d", t=4)
                for q in range(4):
                    for k in range(KD):
                        last = pe.transpose(ps[:, q, P * k:P * k + P], t2[:, k, 4 * n + q], ident_bf[:])
                last.then_inc(prep_filled, 1)
            pe.wait_ge(prep_by_act, 1)
            pe.wait_ge(diag2_ready, 1)
            pe.wait_ge(consts_ready, 9)
            for k in range(KD):
                last = pe.matmul(ps_h[:, 0, P * k:P * k + P], ones[:], diag2[:, k], start=True, stop=True)
            last.then_inc(prep_filled, 1)
            body(0, ffn=False, first=True, skip_s0=True)
            pe.wait_ge(prep_by_dve, 13)
            pe.wait_ge(prep_by_act, 2)
            body(1, ffn=True, head=True)
            with pe.Fori(2, NS - 1) as i:
                body(i, ffn=True)
            body(NS - 1, ffn=True, last=True)
            body(NS, ffn=True, attn=False)


_INS = ['x', 'ctx_768', 'mask_BxS2_bk0', 'g_xattn', 'g_ffn', 'L0_xattn_W_q', 'L0_xattn_W_k', 'L0_xattn_W_v',
        'L0_xattn_W_o', 'L0_xattn_b_o', 'L0_ffn_fast_b', 'L0_ffn_w_fc', 'L0_ffn_w_proj', 'L0_ffn_u', 'L0_ffn_v',
        'L0_ffn_gate']


def kernel(**inputs):
    import numpy as _np
    import concourse.bacc as _bacc
    from concourse import mybir as _mybir
    from concourse.bass_utils import run_bass_kernel_spmd as _run

    nc = _bacc.Bacc("TRN2", target_bir_lowering=False, num_devices=1)
    arrays, args = {}, []
    for name in _INS:
        a = _np.ascontiguousarray(inputs[name])
        if a.ndim == 0:
            a = a.reshape(1)
        arrays[f"in_{name}_dram"] = a
        args.append(nc.dram_tensor(f"in_{name}_dram", a.shape, _mybir.dt.from_np(a.dtype), kind="ExternalInput").ap())
    shape = inputs['x'].shape
    args.append(nc.dram_tensor("out_0_dram", shape, _mybir.dt.float32, kind="ExternalOutput").ap())
    block_kernel(nc, *args)
    r = _run(nc, [arrays], core_ids=[0])
    return r.results[0]["out_0_dram"]
```

```python
from contextlib import ExitStack

import concourse.bass as bass
from concourse import mybir

ALU = mybir.AluOpType
ACT = mybir.ActivationFunctionType
AX = mybir.AxisListType
F32 = mybir.dt.float32
F32R = mybir.dt.float32r
BF16 = mybir.dt.bfloat16
U8 = mybir.dt.uint8

P = 128
LN_EPS = 1e-5
SCALE_FLOOR = 1e-5
MASKED = -3.38e38


def block_kernel(nc, x, context, mask, g_xattn, g_ffn, w_q, w_k, w_v, w_o, b_o, fast_b, w_fc, w_proj,
                 u, v, gate, out):
    B, SEQ, D = x.shape
    J, C = context.shape[1:]
    INNER = w_q.shape[1]
    DH = 64
    HEADS = INNER // DH
    HID = w_fc.shape[0]
    RANK = u.shape[1]
    TT = 4
    TOK = TT * P
    NS = B * SEQ // TOK
    SPB = SEQ // TOK
    KD = D // P
    KI = INNER // P
    KH = HID // P
    HJ = HEADS * J
    HALF = HJ // 2
    BJ = B * J
    KC = (HJ + P - 1) // P
    C1 = C - P
    LASTROWS = HJ - (KC - 1) * P
    ATTN_SCALE = DH ** -0.5
    RING = 4

    ctx = ExitStack()
    with ctx:
        def sb(name, shape, dt=F32):
            return ctx.enter_context(nc.sbuf_tensor(name, shape, dt))

        def sem(name):
            return ctx.enter_context(nc.semaphore(name))

        with ExitStack() as passing:
            def early(name, shape, dt=F32):
                return passing.enter_context(nc.sbuf_tensor(name, shape, dt))

            wq_sb = early("wq_sb", [P, KD, INNER])
            wk_sb = early("wk_sb", [P, 2, INNER])
            wv_sb = early("wv_sb", [P, 2, INNER])
            wo_sb = early("wo_sb", [P, KI, D])
            wqT = early("wqT", [P, KI, D])
            kT = early("kT", [P, HEADS, BJ])
            vT = early("vT", [P, B, KI, 2 * P])
        pT_hi = sb("pT_hi", [P, KC, TOK], F32R)
        pT_lo = sb("pT_lo", [P, KC, TOK], F32R)
        x2nT_hi = sb("x2nT_hi", [P, KD, TOK], F32R)
        x2nT_lo = sb("x2nT_lo", [P, KD, TOK], F32R)
        x2n = sb("x2n", [P, TT, D])
        y_scaled = sb("y_scaled", [P, 2, D])
        with ExitStack() as passing:
            wfc_sb = early("wfc_sb", [P, KH, D])
            wproj_sb = early("wproj_sb", [P, KD, HID])
            below1 = early("below1", [P, KH, D])
            tern1 = early("tern1", [P, KH, D])
            below2 = early("below2", [P, KD, HID], BF16)
            tern2 = early("tern2", [P, KD, HID], BF16)
        r2_hi = sb("r2_hi", [P, KH, TOK], F32R)
        r2_lo = sb("r2_lo", [P, KH, TOK], F32R)
        relu = sb("relu", [P, RING, TOK])
        square = sb("square", [P, RING, TOK])
        x_sb = sb("x_sb", [P, NS, TT, D])
        ctx_sb = sb("ctx_sb", [P, 2, 2 * P])
        bo_row = sb("bo_row", [P, D])
        u_sb = sb("u_sb", [P, KH, RANK])
        v_sb = sb("v_sb", [RANK, D])
        fb_sb = sb("fb_sb", [RANK, RANK])
        gates = sb("gates", [P, 3])
        mask_row = sb("mask_row", [1, B, J], U8)
        ident = sb("ident", [P, P])
        ident_bf = sb("ident_bf", [P, P], BF16)
        ones = sb("ones", [P, P])
        ones_bf = sb("ones_bf", [P, P], BF16)
        head0_rows = sb("head0_rows", [P, P])
        minus_half = sb("minus_half", [P, TT])
        tanh_g = sb("tanh_g", [P, 2])
        ctxT = sb("ctxT", [P, 2, 2 * P])
        a_hi = sb("a_hi", [P, KD, B, HJ], F32R)
        a_lo = sb("a_lo", [P, KD, B, HJ], F32R)
        vo_hi = sb("vo_hi", [P, B * KC, D], F32R)
        vo_lo = sb("vo_lo", [P, B * KC, D], F32R)
        mask_bias = sb("mask_bias", [P, B, HJ], BF16)
        scale1 = sb("scale1", [P, KH, 3])
        scale2 = sb("scale2", [P, KD, 3])
        uT = sb("uT", [RANK, KH, P])
        fbT = sb("fbT", [RANK, RANK])
        bv = sb("bv", [RANK, D])
        w1_hi = sb("w1_hi", [P, KD, KH, P], F32R)
        w1_lo = sb("w1_lo", [P, KD, KH, P], F32R)
        w2T = sb("w2T", [P, KH, D], F32R)
        diag2 = sb("diag2", [P, KD, P])
        col_scale = sb("col_scale", [P, D])
        xn = sb("xn", [P, TT, D])
        xnT_hi = sb("xnT_hi", [P, KD, TOK], F32R)
        xnT_lo = sb("xnT_lo", [P, KD, TOK], F32R)
        stats1 = sb("stats1", [P, TT, 6])
        moments1 = sb("moments1", [P, TT, 2])
        var1 = sb("var1", [P, TT])
        rstd1 = sb("rstd1", [P, TT])
        stats2 = sb("stats2", [P, TT, 6])
        moments2 = sb("moments2", [P, TT, 2])
        var2 = sb("var2", [P, TT])
        rstd2 = sb("rstd2", [P, TT])
        neg_max = sb("neg_max", [P, TT, HEADS])
        row_sum = sb("row_sum", [P, TT, HEADS])
        inv_sum = sb("inv_sum", [P, TT, HEADS])
        probs = sb("probs", [P, TT, HJ])

        ps_s = ctx.enter_context(nc.psum_tensor("ps_s", [P, 2, 512], F32))
        ps_t = ctx.enter_context(nc.psum_tensor("ps_t", [P, 2, 512], F32))
        ps_h = ctx.enter_context(nc.psum_tensor("ps_h", [P, 2, 512], F32))
        ps_o = ctx.enter_context(nc.psum_tensor("ps_o", [P, 2, 512], F32))
        banks = [ps_s[:, 0], ps_s[:, 1], ps_t[:, 0], ps_t[:, 1], ps_h[:, 0], ps_h[:, 1], ps_o[:, 0], ps_o[:, 1]]

        x_in = [sem(f"x_in{s}") for s in range(NS)]
        ctx_in, wq_in, wk_in, wv_in, wo_in, bo_in, mask_in = map(
            sem, ("ctx_in", "wq_in", "wk_in", "wv_in", "wo_in", "bo_in", "mask_in"))
        wfc_in, wproj_in, lowrank_in, gates_in, out_stored = map(
            sem, ("wfc_in", "wproj_in", "lowrank_in", "gates_in", "out_stored"))
        ident_ready, pads_ready, consts_ready, ident_bf_ready, tanh_ready, mask_ready = map(
            sem, ("ident_ready", "pads_ready", "consts_ready", "ident_bf_ready", "tanh_ready", "mask_ready"))
        ctxT_filled, ctxT_ready, wqT_filled, wqT_ready = map(sem, ("ctxT_filled", "ctxT_ready", "wqT_filled", "wqT_ready"))
        k_filled, k_ready, v_filled, v_ready = map(sem, ("k_filled", "k_ready", "v_filled", "v_ready"))
        a_filled, a_hi_done, a_lo_done, vo_filled, vo_hi_done, vo_lo_done = map(
            sem, ("a_filled", "a_hi_done", "a_lo_done", "vo_filled", "vo_hi_done", "vo_lo_done"))
        scale1_done, abs2_done, scale2_done, below1_done, below2_done, tern1_done, tern2_ready, diag2_ready = map(
            sem, ("scale1_done", "abs2_done", "scale2_done", "below1_done", "below2_done", "tern1_done", "tern2_ready",
                  "diag2_ready"))
        uT_filled, uT_ready, fbT_filled, fbT_ready, bv_filled, bv_ready = map(
            sem, ("uT_filled", "uT_ready", "fbT_filled", "fbT_ready", "bv_filled", "bv_ready"))
        lowrank_filled, w1_ready, w1T_filled, w1_hi_done, w1_lo_done, w2T_filled, w2T_ready = map(
            sem, ("lowrank_filled", "w1_ready", "w1T_filled", "w1_hi_done", "w1_lo_done", "w2T_filled", "w2T_ready"))
        col_filled, col_ready = map(sem, ("col_filled", "col_ready"))
        ln1_stats, ln1_moments, ln1_var, ln1_rstd, xn_ready = map(
            sem, ("ln1_stats", "ln1_moments", "ln1_var", "ln1_rstd", "xn_ready"))
        ln2_stats, ln2_moments, ln2_var, ln2_rstd, x2n_ready = map(
            sem, ("ln2_stats", "ln2_moments", "ln2_var", "ln2_rstd", "x2n_ready"))
        t_filled, t_hi_done, t_lo_done = map(sem, ("t_filled", "t_hi_done", "t_lo_done"))
        s_filled, max_done, shifted, exp_done, sum_done, inv_done, p_ready = map(
            sem, ("s_filled", "max_done", "shifted", "exp_done", "sum_done", "inv_done", "p_ready"))
        o_filled, x2_done = map(sem, ("o_filled", "x2_done"))
        h_filled, relu_done, square_done, r2_hi_done, r2_lo_done = map(
            sem, ("h_filled", "relu_done", "square_done", "r2_hi_done", "r2_lo_done"))
        y_filled, y_scaled_done, y_added = map(sem, ("y_filled", "y_scaled_done", "y_added"))

        x_dram = x.rearrange("b (s p t) d -> (b s) p (t d)", p=P, t=TT)
        out_dram = out.rearrange("b (s p t) d -> (b s) p (t d)", p=P, t=TT)
        ctx_dram = context.rearrange("b j c -> (b j) c")

        PER_S = KC + 2 * KD

        def probs_fill(i, c):
            return KD + PER_S * i + c

        def ln1_fill(i, k):
            return KD + PER_S * i + KC + k

        def ln2_fill(i, k, last):
            return KD + PER_S * i + KC + k + (0 if last else KD)

        def batch(i):
            return i // SPB

        def attn_bank(t, ffn):
            return (0, 0, 1, 0)[t] if ffn else t % 2

        def ffn_bank(t, attn):
            return (0, 1, 1, 1)[t] if attn else t % 2

        block = ctx.enter_context(nc.Block())

        @block.sync
        def _(sp):
            sp.wait_ge(pads_ready, 1)
            sp.dma_start(ctx_sb[:, 0, 0:C], ctx_dram[0:P, :]).then_inc(ctx_in, 16)
            sp.dma_start(ctx_sb[0:BJ - P, 1, 0:C], ctx_dram[P:BJ, :]).then_inc(ctx_in, 16)
            sp.dma_start(wk_sb[:, 0, :], w_k[0:P, :]).then_inc(wk_in, 16)
            sp.dma_start(wk_sb[0:C1, 1, :], w_k[P:C, :]).then_inc(wk_in, 16)
            sp.dma_start(wq_sb[:], w_q.rearrange("(k p) n -> p k n", p=P)).then_inc(wq_in, 16)
            sp.dma_start(wv_sb[:, 0, :], w_v[0:P, :]).then_inc(wv_in, 16)
            sp.dma_start(wv_sb[0:C1, 1, :], w_v[P:C, :]).then_inc(wv_in, 16)
            sp.dma_start(wo_sb[:], w_o.rearrange("(k p) n -> p k n", p=P)).then_inc(wo_in, 16)
            sp.wait_ge(pads_ready, 2)
            sp.dma_start(bo_row[0:1, :], b_o.rearrange("(a d) -> a d", a=1)).then_inc(bo_in, 16)
            sp.dma_start(wproj_sb[:], w_proj.rearrange("(k p) n -> p k n", p=P)).then_inc(wproj_in, 16)
            for s in range(1, NS):
                sp.dma_start(x_sb[:, s].rearrange("p t d -> p (t d)"), x_dram[s]).then_inc(x_in[s], 16)
            with sp.Fori(0, NS - 1) as s:
                sp.wait_ge(y_added, TT * s + TT)
                sp.dma_start(out_dram[s], x_sb[:, s].rearrange("p t d -> p (t d)")).then_inc(out_stored, 16)
            for t in range(TT):
                sp.wait_ge(y_added, TT * (NS - 1) + t + 1)
                sp.dma_start(out_dram[NS - 1, :, t * D:(t + 1) * D], x_sb[:, NS - 1, t]).then_inc(out_stored, 16)
            sp.wait_ge(out_stored, 16 * (NS - 1 + TT))

        @block.gpsimd
        def _(pool):
            pool.memset(ctx_sb[:], 0.0).then_inc(pads_ready, 1)
            pool.memset(ident[:], 0.0).then_inc(consts_ready, 1)
            pool.wait_ge(consts_ready, 1)
            pool.affine_select(out=ident[:], in_=ident[:], compare_op=ALU.not_equal, fill=1.0, base=0,
                               pattern=[[-1, P]], channel_multiplier=1).then_inc(ident_ready, 1)
            pool.memset(bo_row[:], 0.0).then_inc(pads_ready, 1)
            pool.memset(minus_half[:], -0.5).then_inc(consts_ready, 1)
            pool.memset(kT[:], 0.0).then_inc(consts_ready, 1)
            pool.memset(mask_bias[:], 0.0).then_inc(consts_ready, 1)
            pool.memset(ones_bf[:], 1.0).then_inc(consts_ready, 1)
            pool.memset(head0_rows[:], 0.0).then_inc(consts_ready, 1)
            pool.wait_ge(consts_ready, 6)
            pool.memset(head0_rows[0:1, 0:J], 1.0).then_inc(consts_ready, 1)
            pool.memset(vT[:], 0.0).then_inc(consts_ready, 1)
            pool.memset(ones[:], 1.0).then_inc(consts_ready, 1)

            def rstd1_step(i):
                pool.wait_ge(ln1_var, i + 1)
                pool.tensor_tensor(rstd1[:], var1[:], minus_half[:], ALU.pow).then_inc(ln1_rstd, 1)

            def rstd2_step(i, half):
                pool.wait_ge(ln2_var, 2 * i + half + 1)
                pool.tensor_tensor(rstd2[:, 2 * half:2 * half + 2], var2[:, 2 * half:2 * half + 2],
                                   minus_half[:, 0:2], ALU.pow).then_inc(ln2_rstd, 1)

            def normalise(i, t):
                pool.wait_ge(inv_done, TT * i + t + 1)
                p3 = probs[:, t].rearrange("p (h j) -> p h j", h=HEADS)
                pool.tensor_tensor(p3, p3, inv_sum[:, t].unsqueeze(2).to_broadcast([P, HEADS, J]),
                                   ALU.mult).then_inc(p_ready, 1)

            def square_step(f, m, head=False):
                pool.wait_ge(relu_done, KH * f + m + 1)
                if not (head and m < RING):
                    pool.wait_ge(r2_lo_done, KH * f + m - RING + 1)
                pool.tensor_tensor(square[:, m % RING], relu[:, m % RING], relu[:, m % RING],
                                   ALU.mult).then_inc(square_done, 1)

            def add_step(f, t):
                pool.wait_ge(y_scaled_done, TT * f + t + 1)
                pool.tensor_tensor(x_sb[:, f, t], y_scaled[:, t % 2], x_sb[:, f, t], ALU.add).then_inc(y_added, 1)

            pool.wait_ge(mask_in, 16)
            pool.wait_ge(consts_ready, 4)
            for h in range(HEADS):
                last = pool.tensor_scalar(mask_bias[0:1, :, h * J:(h + 1) * J], mask_row[:], -1.0, -MASKED,
                                          ALU.add, ALU.mult)
            last.then_inc(mask_ready, 1)
            rstd1_step(0)

            def below1_step(t):
                pool.wait_ge(scale1_done, 3)
                pool.tensor_scalar(below1[:, t], wfc_sb[:, t], scale1[:, t, 2:3], None, ALU.is_lt).then_inc(below1_done, 1)

            def below2_step(k):
                pool.wait_ge(scale2_done, 2)
                pool.tensor_scalar(below2[:, k], wproj_sb[:, k], scale2[:, k, 2:3], None, ALU.is_lt).then_inc(below2_done, 1)

            for t in range(KH):
                below1_step(t)
            normalise(0, 0)
            normalise(0, 1)
            below2_step(0)
            normalise(0, 2)
            below2_step(1)
            normalise(0, 3)
            rstd1_step(1)
            rstd2_step(0, 0)
            rstd2_step(0, 1)

            def both(i, last=False, head=False):
                f = i - 1
                square_step(f, 0, head)
                square_step(f, 1, head)
                normalise(i, 0)
                square_step(f, 2, head)
                square_step(f, 3, head)
                normalise(i, 1)
                square_step(f, 4)
                normalise(i, 2)
                square_step(f, 5)
                normalise(i, 3)
                square_step(f, 6)
                square_step(f, 7)
                if not last:
                    rstd1_step(i + 1)
                add_step(f, 0)
                add_step(f, 1)
                add_step(f, 2)
                rstd2_step(i, 0)
                rstd2_step(i, 1)
                add_step(f, 3)

            both(1, head=True)
            with pool.Fori(2, NS - 1) as i:
                both(i)
            both(NS - 1, last=True)
            for m in range(KH):
                square_step(NS - 1, m)
            for t in range(TT):
                add_step(NS - 1, t)

        @block.scalar
        def _(act):
            act.dma_start(x_sb[:, 0].rearrange("p t d -> p (t d)"), x_dram[0]).then_inc(x_in[0], 16)
            act.dma_start(mask_row[:], mask.rearrange("(a b) j -> a b j", a=1)).then_inc(mask_in, 16)
            act.dma_start(wfc_sb[:], w_fc.rearrange("(p t) d -> p t d", t=KH)).then_inc(wfc_in, 16)
            for n, g in enumerate((g_xattn, g_ffn, gate)):
                act.dma_start(gates[:, n:n + 1],
                              g.rearrange("(a b) -> a b", a=1).to_broadcast([P, 1])).then_inc(gates_in, 16)
            act.dma_start(u_sb[:], u.rearrange("(p t) r -> p t r", t=KH)).then_inc(lowrank_in, 16)
            act.dma_start(v_sb[:], v).then_inc(lowrank_in, 16)
            act.dma_start(fb_sb[:], fast_b).then_inc(lowrank_in, 16)

            act.wait_ge(consts_ready, 2)
            act.activation(tanh_g[:, 0:1], minus_half[:, 0:1], ACT.Tanh)
            act.wait_ge(ctxT_filled, 1)
            act.activation(ctxT[:], banks[0].rearrange("p (k n) -> p k n", k=2), ACT.Identity).then_inc(ctxT_ready, 1)
            for n in range(2):
                act.wait_ge(wqT_filled, n + 1)
                act.activation(wqT[:, 2 * n:2 * n + 2], banks[1 + n].rearrange("p (c d) -> p c d", c=2),
                               ACT.Identity).then_inc(wqT_ready, 1)
            act.wait_ge(consts_ready, 3)
            for n in range(2):
                act.wait_ge(k_filled, n + 1)
                ps = banks[3 + n].rearrange("p (c n) -> p c n", c=2)[:, :, 0:BJ]
                to = kT[:, 4 * n:4 * n + 4].rearrange("p (c e) n -> p c e n", e=2)
                for e in range(2):
                    rows = slice(DH * e, DH * e + DH)
                    last = act.activation(to[rows, :, e], ps[rows], ACT.Identity, scale=ATTN_SCALE)
                last.then_inc(k_ready, 1)
            for n in range(KD * KI):
                m, c = divmod(n, KI)
                act.wait_ge(a_filled, n + 1)
                act.activation(a_hi[:, m, :, 2 * c * J:2 * (c + 1) * J].rearrange("p b (h j) -> p h b j", h=2),
                               banks[(5 + n) % 8][:, 0:2 * BJ].rearrange("p (h b j) -> p h b j", h=2, b=B),
                               ACT.Identity).then_inc(a_hi_done, 1)

            def split_hi(f, k, to):
                act.wait_ge(t_filled, f + 1)
                act.activation(to, k, ACT.Identity).then_inc(t_hi_done, 1)

            def split_ln(fill, to):
                for k in range(KD):
                    split_hi(fill(k), ps_t[:, (1 + k) % 2], to[:, k])

            def split_probs(i, c):
                split_hi(probs_fill(i, c), ps_t[:, c % 2], pT_hi[:, c])

            def exp_step(i, t):
                act.wait_ge(shifted, TT * i + t + 1)
                act.activation(probs[:, t], probs[:, t], ACT.Exp).then_inc(exp_done, 1)

            def relu_step(f, m, head=False):
                act.wait_ge(h_filled, KH * f + m + 1)
                if not (head and m < RING):
                    act.wait_ge(square_done, KH * f + m - RING + 1)
                act.activation(relu[:, m % RING], ps_h[:, m % 2], ACT.Relu).then_inc(relu_done, 1)

            def square_hi(f, m):
                act.wait_ge(relu_done, KH * f + m + 1)
                act.activation(r2_hi[:, m], relu[:, m % RING], ACT.Square).then_inc(r2_hi_done, 1)

            split_ln(lambda k: k, xnT_hi)
            act.wait_ge(consts_ready, 8)
            for n in range(2):
                act.wait_ge(v_filled, n + 1)
                for c in (2 * n, 2 * n + 1):
                    for e in range(2):
                        rows, at = slice(DH * e, DH * e + DH), (2 * c + e) * J - P * c
                        last = act.activation(vT[rows, :, c, at:at + J],
                                              banks[5 + n][rows, 256 * (c % 2):256 * (c % 2) + BJ].rearrange("p (b j) -> p b j", b=B),
                                              ACT.Identity)
                last.then_inc(v_ready, 1)
            act.wait_ge(gates_in, 48)
            act.activation(tanh_g[:], gates[:, 0:2], ACT.Tanh).then_inc(tanh_ready, 1)
            exp_step(0, 0)
            act.wait_ge(tanh_ready, 1)
            for n in range(B * KC // 2):
                act.wait_ge(vo_filled, n + 1)
                act.activation(vo_hi[:, 2 * n:2 * n + 2], banks[(7, 4, 5, 6, 7)[n]].rearrange("p (k d) -> p k d", k=2),
                               ACT.Identity, scale=tanh_g[:, 0:1]).then_inc(vo_hi_done, 1)
            act.wait_ge(wproj_in, 16)
            for k in range(KD):
                act.activation(tern2[:, k], wproj_sb[:, k], ACT.Abs, accum_out=scale2[:, k, 0:1]).then_inc(abs2_done, 1)
            exp_step(0, 1)
            for n in range(2):
                act.wait_ge(uT_filled, n + 1)
                act.activation(uT[:, 4 * n:4 * n + 4], ps_h[0:RANK, n].rearrange("r (t p) -> r t p", t=4),
                               ACT.Identity, scale=gates[0:RANK, 2:3]).then_inc(uT_ready, 1)
            act.wait_ge(fbT_filled, 1)
            act.activation(fbT[:], ps_h[0:RANK, 0, 0:RANK], ACT.Identity).then_inc(fbT_ready, 1)
            act.wait_ge(bv_filled, 1)
            act.activation(bv[:], ps_h[0:RANK, 1, 0:D], ACT.Identity).then_inc(bv_ready, 1)
            exp_step(0, 2)
            exp_step(0, 3)
            for n in range(KD * KH // 4):
                act.wait_ge(w1T_filled, n + 1)
                act.activation(w1_hi[:, n // 2, 4 * (n % 2):4 * (n % 2) + 4],
                               ps_h[:, n % 2].rearrange("p (t n) -> p t n", t=4), ACT.Identity).then_inc(w1_hi_done, 1)
            for c in range(KC):
                split_probs(0, c)
            for n in range(2):
                act.wait_ge(w2T_filled, n + 1)
                act.activation(w2T[:, 4 * n:4 * n + 4], ps_h[:, n].bitcast(BF16).rearrange("p (t d) -> p t d", t=4),
                               ACT.Identity).then_inc(w2T_ready, 1)
            split_ln(lambda k: ln1_fill(0, k), xnT_hi)
            split_ln(lambda k: ln2_fill(0, k, False), x2nT_hi)

            def both(i, last=False, head=False):
                f = i - 1
                relu_step(f, 0, head)
                exp_step(i, 0)
                square_hi(f, 0)
                relu_step(f, 1, head)
                square_hi(f, 1)
                relu_step(f, 2, head)
                exp_step(i, 1)
                square_hi(f, 2)
                relu_step(f, 3, head)
                square_hi(f, 3)
                relu_step(f, 4)
                exp_step(i, 2)
                square_hi(f, 4)
                relu_step(f, 5)
                exp_step(i, 3)
                square_hi(f, 5)
                relu_step(f, 6)
                square_hi(f, 6)
                relu_step(f, 7)
                square_hi(f, 7)
                for c in range(KC):
                    split_probs(i, c)
                if not last:
                    split_ln(lambda k: ln1_fill(i, k), xnT_hi)
                split_ln(lambda k: ln2_fill(i, k, last), x2nT_hi)

            both(1, head=True)
            with act.Fori(2, NS - 1) as i:
                both(i)
            both(NS - 1, last=True)
            for m in range(KH):
                relu_step(NS - 1, m)
                square_hi(NS - 1, m)

        @block.vector
        def _(dve):
            def settled():
                dve.wait_ge(ident_ready, 1)

            def ln1_stats_step(i, t):
                settled()
                dve.bn_stats(stats1[:, t], x_sb[:, i, t]).then_inc(ln1_stats, 1)

            def ln1_moments_step(i):
                dve.wait_ge(ln1_stats, TT * i + TT)
                settled()
                for t in range(TT):
                    last = dve.bn_aggr(moments1[:, t], stats1[:, t])
                last.then_inc(ln1_moments, 1)
                dve.wait_ge(ln1_moments, i + 1)
                dve.tensor_scalar(var1[:], moments1[:, :, 1], LN_EPS, None, ALU.add).then_inc(ln1_var, 1)

            def ln1_normalise(i):
                dve.wait_ge(ln1_rstd, i + 1)
                for t in range(TT):
                    last = dve.tensor_scalar(xn[:, t], x_sb[:, i, t], moments1[:, t, 0:1], rstd1[:, t:t + 1],
                                             ALU.subtract, ALU.mult)
                last.then_inc(xn_ready, 1)

            def residual(i, t, ffn=True):
                dve.wait_ge(o_filled, TT * i + t + 1)
                dve.tensor_tensor(x_sb[:, i, t], ps_o[:, attn_bank(t, ffn), 0:D], x_sb[:, i, t], ALU.add).then_inc(x2_done, 1)
                dve.wait_ge(x2_done, TT * i + t + 1)
                settled()
                dve.bn_stats(stats2[:, t], x_sb[:, i, t]).then_inc(ln2_stats, 1)
                dve.wait_ge(ln2_stats, TT * i + t + 1)
                settled()
                dve.bn_aggr(moments2[:, t], stats2[:, t]).then_inc(ln2_moments, 1)

            def ln2_var_step(i, half):
                dve.wait_ge(ln2_moments, TT * i + 2 * half + 2)
                dve.tensor_scalar(var2[:, 2 * half:2 * half + 2], moments2[:, 2 * half:2 * half + 2, 1], LN_EPS,
                                  None, ALU.add).then_inc(ln2_var, 1)

            def ln2_normalise(i, half):
                dve.wait_ge(ln2_rstd, 2 * i + half + 1)
                for t in (2 * half, 2 * half + 1):
                    last = dve.tensor_scalar(x2n[:, t], x_sb[:, i, t], moments2[:, t, 0:1], rstd2[:, t:t + 1],
                                             ALU.subtract, ALU.mult)
                last.then_inc(x2n_ready, 1)

            def split_lo(f, ps, hi, lo):
                dve.wait_ge(t_hi_done, f + 1)
                dve.tensor_tensor(lo, ps, hi.bitcast(F32), ALU.subtract).then_inc(t_lo_done, 1)

            def split_probs(i, c):
                split_lo(probs_fill(i, c), ps_t[:, c % 2], pT_hi[:, c], pT_lo[:, c])

            def split_xn(i, k):
                split_lo(ln1_fill(i, k), ps_t[:, (1 + k) % 2], xnT_hi[:, k], xnT_lo[:, k])

            def split_x2n(i, k, last=False):
                split_lo(ln2_fill(i, k, last), ps_t[:, (1 + k) % 2], x2nT_hi[:, k], x2nT_lo[:, k])

            heads4 = ps_s[:, :, 0:HALF].rearrange("p b (h j) -> p b h j", h=HEADS // 2)

            def shift_step(i, t):
                dve.wait_ge(s_filled, TT * i + t + 1)
                dve.tensor_reduce(neg_max[:, t], heads4, AX.X, ALU.max, negate=True).then_inc(max_done, 1)
                dve.wait_ge(max_done, TT * i + t + 1)
                shift = neg_max[:, t].rearrange("p (b h) -> p b h", b=2).unsqueeze(3).to_broadcast([P, 2, HEADS // 2, J])
                dve.tensor_tensor(probs[:, t].rearrange("p (b h j) -> p b h j", b=2, h=HEADS // 2), heads4, shift,
                                  ALU.add).then_inc(shifted, 1)

            def sum_step(i, t):
                dve.wait_ge(exp_done, TT * i + t + 1)
                dve.tensor_reduce(row_sum[:, t], probs[:, t].rearrange("p (h j) -> p h j", h=HEADS), AX.X,
                                  ALU.add).then_inc(sum_done, 1)
                dve.wait_ge(sum_done, TT * i + t + 1)
                dve.reciprocal(inv_sum[:, t], row_sum[:, t]).then_inc(inv_done, 1)

            def split_square(f, m):
                dve.wait_ge(square_done, KH * f + m + 1)
                dve.wait_ge(r2_hi_done, KH * f + m + 1)
                dve.tensor_tensor(r2_lo[:, m], square[:, m % RING], r2_hi[:, m].bitcast(F32),
                                  ALU.subtract).then_inc(r2_lo_done, 1)

            def y_step(f, t, attn=True, head=False):
                dve.wait_ge(y_filled, TT * f + t + 1)
                if not (head and t < 2):
                    dve.wait_ge(y_added, TT * f + t - 1)
                dve.tensor_tensor(y_scaled[:, t % 2], ps_o[:, ffn_bank(t, attn), 0:D], col_scale[:],
                                  ALU.mult).then_inc(y_scaled_done, 1)

            dve.wait_ge(x_in[0], 16)
            for t in range(TT):
                ln1_stats_step(0, t)
            ln1_moments_step(0)
            dve.wait_ge(wfc_in, 16)
            dve.tensor_reduce(scale1[:, :, 0], wfc_sb[:], AX.X, ALU.add, apply_absolute_value=True).then_inc(scale1_done, 1)
            ln1_normalise(0)
            dve.wait_ge(scale1_done, 1)
            dve.tensor_scalar(scale1[:, :, 0], scale1[:, :, 0], 1.0 / D, SCALE_FLOOR, ALU.mult, ALU.max).then_inc(scale1_done, 1)
            dve.wait_ge(scale1_done, 2)
            dve.tensor_scalar(scale1[:, :, 1], scale1[:, :, 0], 0.5, None, ALU.mult)
            dve.tensor_scalar(scale1[:, :, 2], scale1[:, :, 0], -0.5, None, ALU.mult).then_inc(scale1_done, 1)
            dve.tensor_copy(ident_bf[:], ident[:]).then_inc(ident_bf_ready, 1)
            for n in range(KD * KI):
                m, c = divmod(n, KI)
                dve.wait_ge(a_hi_done, n + 1)
                view = [a[:, m, :, 2 * c * J:2 * (c + 1) * J].rearrange("p b (h j) -> p h b j", h=2) for a in (a_lo, a_hi)]
                dve.tensor_tensor(view[0], banks[(5 + n) % 8][:, 0:2 * BJ].rearrange("p (h b j) -> p h b j", h=2, b=B),
                                  view[1].bitcast(F32), ALU.subtract).then_inc(a_lo_done, 1)
            for k in range(KD):
                split_lo(k, ps_t[:, (1 + k) % 2], xnT_hi[:, k], xnT_lo[:, k])

            def ternary1(t):
                dve.wait_ge(below1_done, t + 1)
                dve.scalar_tensor_tensor(out=tern1[:, t], in0=wfc_sb[:, t], scalar=scale1[:, t, 1:2], in1=below1[:, t],
                                         op0=ALU.is_gt, op1=ALU.subtract).then_inc(tern1_done, 1)

            shift_step(0, 0)
            dve.wait_ge(tanh_ready, 1)
            for n in range(B * KC // 2):
                dve.wait_ge(vo_hi_done, n + 1)
                dve.scalar_tensor_tensor(out=vo_lo[:, 2 * n:2 * n + 2],
                                         in0=banks[(7, 4, 5, 6, 7)[n]].rearrange("p (k d) -> p k d", k=2),
                                         scalar=tanh_g[:, 0:1], in1=vo_hi[:, 2 * n:2 * n + 2].bitcast(F32),
                                         op0=ALU.mult, op1=ALU.subtract).then_inc(vo_lo_done, 1)
                if n == 0:
                    sum_step(0, 0)
            shift_step(0, 1)
            for t in range(KH // 2):
                ternary1(t)
            sum_step(0, 1)
            for t in range(KH // 2, KH):
                ternary1(t)
            dve.wait_ge(abs2_done, KD)
            dve.tensor_scalar(scale2[:, :, 0], scale2[:, :, 0], 1.0 / HID, SCALE_FLOOR, ALU.mult, ALU.max).then_inc(scale2_done, 1)
            shift_step(0, 2)
            dve.wait_ge(scale2_done, 1)
            dve.tensor_scalar(scale2[:, :, 1], scale2[:, :, 0], 0.5, None, ALU.mult)
            dve.tensor_scalar(scale2[:, :, 2], scale2[:, :, 0], -0.5, None, ALU.mult).then_inc(scale2_done, 1)
            for n in range(KH // 2):
                if n == 1:
                    sum_step(0, 2)
                if n == 2:
                    shift_step(0, 3)
                dve.wait_ge(lowrank_filled, n + 1)
                for t in (2 * n, 2 * n + 1):
                    dve.wait_ge(tern1_done, t + 1)
                    last = dve.scalar_tensor_tensor(out=wfc_sb[:, t], in0=tern1[:, t], scalar=scale1[:, t, 0:1],
                                                    in1=ps_h[:, n % 2, D * (t % 2):D * (t % 2) + D],
                                                    op0=ALU.mult, op1=ALU.add)
                last.then_inc(w1_ready, 1)
            sum_step(0, 3)
            for n in range(KD * KH // 4):
                dve.wait_ge(w1_hi_done, n + 1)
                to = [w[:, n // 2, 4 * (n % 2):4 * (n % 2) + 4] for w in (w1_lo, w1_hi)]
                dve.tensor_tensor(to[0], ps_h[:, n % 2].rearrange("p (t n) -> p t n", t=4), to[1].bitcast(F32),
                                  ALU.subtract).then_inc(w1_lo_done, 1)
            for k in range(KD):
                last = dve.tensor_scalar(diag2[:, k], ident[:], scale2[:, k, 0:1], tanh_g[:, 1:2], ALU.mult, ALU.mult)
            last.then_inc(diag2_ready, 1)

            def ternary2(k):
                dve.wait_ge(below2_done, k + 1)
                dve.scalar_tensor_tensor(out=tern2[:, k], in0=wproj_sb[:, k], scalar=scale2[:, k, 1:2], in1=below2[:, k],
                                         op0=ALU.is_gt, op1=ALU.subtract).then_inc(tern2_ready, 1)

            split_probs(0, 0)
            split_probs(0, 1)
            ternary2(0)
            split_probs(0, 2)
            split_probs(0, 3)
            ternary2(1)
            split_probs(0, 4)
            for s in range(1, NS):
                dve.wait_ge(x_in[s], 16)
            for t in range(TT):
                ln1_stats_step(1, t)
            ln1_moments_step(1)
            residual(0, 0, ffn=False)
            residual(0, 1, ffn=False)
            ln2_var_step(0, 0)
            ln1_normalise(1)
            residual(0, 2, ffn=False)
            ln2_normalise(0, 0)
            residual(0, 3, ffn=False)
            ln2_var_step(0, 1)
            split_xn(0, 0)
            ln2_normalise(0, 1)
            split_xn(0, 1)
            dve.wait_ge(col_filled, 1)
            dve.tensor_copy(col_scale[:], ps_h[:, 0, 0:D]).then_inc(col_ready, 1)
            split_x2n(0, 0)
            split_x2n(0, 1)

            def both(i, last=False, head=False):
                f = i - 1
                shift_step(i, 0)
                if not last:
                    ln1_stats_step(i + 1, 0)
                sum_step(i, 0)
                split_square(f, 0)
                shift_step(i, 1)
                if not last:
                    ln1_stats_step(i + 1, 1)
                split_square(f, 1)
                sum_step(i, 1)
                split_square(f, 2)
                shift_step(i, 2)
                split_square(f, 3)
                if not last:
                    ln1_stats_step(i + 1, 2)
                sum_step(i, 2)
                shift_step(i, 3)
                split_square(f, 4)
                if not last:
                    ln1_stats_step(i + 1, 3)
                sum_step(i, 3)
                if not last:
                    ln1_moments_step(i + 1)
                split_square(f, 5)
                split_square(f, 6)
                split_probs(i, 0)
                split_square(f, 7)
                split_probs(i, 1)
                y_step(f, 0, head=head)
                split_probs(i, 2)
                split_probs(i, 3)
                y_step(f, 1, head=head)
                split_probs(i, 4)
                if not last:
                    ln1_normalise(i + 1)
                residual(i, 0)
                y_step(f, 2)
                residual(i, 1)
                ln2_var_step(i, 0)
                residual(i, 2)
                ln2_normalise(i, 0)
                residual(i, 3)
                ln2_var_step(i, 1)
                if not last:
                    split_xn(i, 0)
                ln2_normalise(i, 1)
                if not last:
                    split_xn(i, 1)
                y_step(f, 3)
                split_x2n(i, 0, last)
                split_x2n(i, 1, last)

            both(1, head=True)
            with dve.Fori(2, NS - 1) as i:
                both(i)
            both(NS - 1, last=True)
            for m in range(KH):
                split_square(NS - 1, m)
            for t in range(TT):
                y_step(NS - 1, t, attn=False)

        @block.tensor
        def _(pe):
            pe.wait_ge(ident_ready, 1)
            pe.wait_ge(ctx_in, 32)
            for k in range(2):
                for r in range(2):
                    last = pe.transpose(banks[0][:, 256 * k + P * r:256 * k + P * r + P],
                                        ctx_sb[:, r, P * k:P * k + P], ident[:])
            last.then_inc(ctxT_filled, 1)

            def project_context(bank, w, c):
                pe.matmul(bank[:, 0:BJ], w[:, 0, P * c:P * c + P], ctxT[:, 0, 0:BJ], start=True, stop=False)
                return pe.matmul(bank[:, 0:BJ], w[0:C1, 1, P * c:P * c + P], ctxT[0:C1, 1, 0:BJ],
                                 start=False, stop=True)

            pe.wait_ge(wq_in, 16)
            for n in range(2):
                for c in range(2):
                    for k in range(KD):
                        cc = 2 * n + c
                        last = pe.transpose(banks[1 + n][:, 256 * c + P * k:256 * c + P * k + P],
                                            wq_sb[:, k, P * cc:P * cc + P], ident[:])
                last.then_inc(wqT_filled, 1)
            pe.wait_ge(ctxT_ready, 1)
            pe.wait_ge(wk_in, 32)
            for n in range(2):
                for c in range(2):
                    last = project_context(banks[3 + n][:, 256 * c:256 * c + 256], wk_sb, 2 * n + c)
                last.then_inc(k_filled, 1)
            pe.wait_ge(wqT_ready, 2)
            for n in range(KD * KI):
                m, c = divmod(n, KI)
                pe.wait_ge(k_ready, c // 2 + 1)
                pe.matmul(banks[(5 + n) % 8][:, 0:2 * BJ], wqT[:, c, P * m:P * m + P], kT[:, 2 * c:2 * c + 2, :],
                          start=True, stop=True).then_inc(a_filled, 1)
            pe.wait_ge(wv_in, 32)
            for n in range(2):
                pe.wait_ge(a_lo_done, n + 1)
                for c in range(2):
                    last = project_context(banks[5 + n][:, 256 * c:256 * c + 256], wv_sb, 2 * n + c)
                last.then_inc(v_filled, 1)

            def transpose_ln(src, fill):
                for k in range(KD):
                    if fill(k) is not None:
                        pe.wait_ge(t_lo_done, fill(k) - 1)
                    for t in range(TT):
                        last = pe.transpose(ps_t[:, (1 + k) % 2, P * t:P * t + P], src[:, t, P * k:P * k + P], ident[:])
                    last.then_inc(t_filled, 1)

            def transpose_probs(i, c):
                if c == 0:
                    pe.wait_ge(p_ready, TT * i + TT)
                pe.wait_ge(t_lo_done, probs_fill(i, c) - {0: 0, 1: 2}.get(c, 1))
                rows = P if c < KC - 1 else LASTROWS
                for t in range(TT):
                    last = pe.transpose(ps_t[0:rows, c % 2, P * t:P * t + P], probs[:, t, P * c:P * c + rows], ident[:])
                last.then_inc(t_filled, 1)

            def scores(i, t, first=False):
                if not first:
                    pe.wait_ge(shifted, TT * i + t)
                for half in range(2):
                    cols = slice(HALF * half, HALF * half + HALF)
                    ps = ps_s[:, half, 0:HALF]
                    pe.matmul(ps, ones_bf[:], mask_bias[:, batch(i), cols], start=True, stop=False)
                    for k in range(KD):
                        hi, lo = xnT_hi[:, k, P * t:P * t + P], xnT_lo[:, k, P * t:P * t + P]
                        pe.matmul(ps, hi, a_hi[:, k, batch(i), cols], start=False, stop=False)
                        pe.matmul(ps, hi, a_lo[:, k, batch(i), cols], start=False, stop=False)
                        last = pe.matmul(ps, lo, a_hi[:, k, batch(i), cols], start=False, stop=(k == KD - 1))
                last.then_inc(s_filled, 1)

            def attend(i, t, ffn=True):
                if ffn and t % 2 == 0:
                    pe.wait_ge(y_scaled_done, TT * (i - 1) + t + 1)
                elif ffn or t >= 2:
                    pe.wait_ge(x2_done, TT * i + (t // 2 + 1 if ffn else t - 1))
                ps = ps_o[:, attn_bank(t, ffn), 0:D]
                for c in range(KC):
                    if t == 0:
                        pe.wait_ge(t_lo_done, probs_fill(i, c) + 1)
                    rows = P if c < KC - 1 else LASTROWS
                    hi, lo = pT_hi[0:rows, c, P * t:P * t + P], pT_lo[0:rows, c, P * t:P * t + P]
                    at = batch(i) * KC + c
                    pe.matmul(ps, hi, vo_hi[0:rows, at], start=(c == 0), stop=False)
                    pe.matmul(ps, hi, vo_lo[0:rows, at], start=False, stop=False)
                    last = pe.matmul(ps, lo, vo_hi[0:rows, at], start=False, stop=(c == KC - 1))
                last.then_inc(o_filled, 1)

            def hidden(f, m, head=False):
                if not (head and m < 2):
                    pe.wait_ge(relu_done, KH * f + m - 1)
                ps = ps_h[:, m % 2]
                for k in range(KD):
                    pe.matmul(ps, w1_hi[:, k, m], x2nT_hi[:, k], start=(k == 0), stop=False)
                    pe.matmul(ps, w1_lo[:, k, m], x2nT_hi[:, k], start=False, stop=False)
                    last = pe.matmul(ps, w1_hi[:, k, m], x2nT_lo[:, k], start=False, stop=(k == KD - 1))
                last.then_inc(h_filled, 1)

            def project_out(f, t, attn=True, head=False):
                if t == 0:
                    pe.wait_ge(x2_done, TT * f + TT + (0 if attn else 0))
                elif t == 1 and not head:
                    pe.wait_ge(y_scaled_done, TT * f)
                elif t == 2:
                    pe.wait_ge(y_scaled_done, TT * f + (2 if attn else 1))
                elif t == 3 and attn:
                    pe.wait_ge(x2_done, TT * f + TT + 3)
                elif t == 3:
                    pe.wait_ge(y_scaled_done, TT * f + 2)
                ps = ps_o[:, ffn_bank(t, attn), 0:D]
                for m in range(KH):
                    if t == 0:
                        pe.wait_ge(r2_lo_done, KH * f + m + 1)
                    pe.matmul(ps, r2_hi[:, m, P * t:P * t + P], w2T[:, m], start=(m == 0), stop=False)
                    last = pe.matmul(ps, r2_lo[:, m, P * t:P * t + P], w2T[:, m],
                                     start=False, stop=(m == KH - 1))
                last.then_inc(y_filled, 1)

            pe.wait_ge(a_lo_done, KD * KI)
            pe.wait_ge(xn_ready, 1)
            transpose_ln(xn, lambda k: None if k < 2 else k)
            pe.wait_ge(t_lo_done, KD)
            pe.wait_ge(mask_ready, 1)
            scores(0, 0, first=True)
            pe.wait_ge(v_ready, 2)
            pe.wait_ge(wo_in, 16)
            pe.wait_ge(bo_in, 16)
            for n in range(B * KC // 2):
                if n == 4:
                    pe.wait_ge(vo_lo_done, 1)
                for q in range(2):
                    b, tile = divmod(2 * n + q, KC)
                    ps = banks[(7, 4, 5, 6, 7)[n]][:, D * q:D * q + D]
                    terms = [(vT[:, b, c, P * (tile - c):P * (tile - c) + P], wo_sb[:, c]) for c in (tile - 1, tile)
                             if 0 <= c < KI]
                    if tile == 0:
                        terms.append((head0_rows[:], bo_row[:]))
                    for at, (lhsT, rhs) in enumerate(terms):
                        last = pe.matmul(ps, lhsT, rhs, start=(at == 0), stop=(at == len(terms) - 1))
                last.then_inc(vo_filled, 1)
            scores(0, 1)
            pe.wait_ge(lowrank_in, 48)
            for n in range(2):
                pe.wait_ge(vo_lo_done, 2 + n)
                for t in range(4):
                    last = pe.matmul(ps_h[0:RANK, n, P * t:P * t + P], u_sb[:, 4 * n + t], ident[:], start=True, stop=True)
                last.then_inc(uT_filled, 1)
            pe.wait_ge(uT_ready, 1)
            pe.matmul(ps_h[0:RANK, 0, 0:RANK], fb_sb[:], ident[0:RANK, 0:RANK], start=True, stop=True).then_inc(fbT_filled, 1)
            pe.wait_ge(uT_ready, 2)
            pe.wait_ge(fbT_ready, 1)
            pe.matmul(ps_h[0:RANK, 1, 0:D], fbT[:], v_sb[:], start=True, stop=True).then_inc(bv_filled, 1)
            scores(0, 2)
            pe.wait_ge(bv_ready, 1)
            for n in range(KH // 2):
                if n == 2:
                    scores(0, 3)
                if n >= 2:
                    pe.wait_ge(w1_ready, n - 1)
                for q in range(2):
                    last = pe.matmul(ps_h[:, n % 2, D * q:D * q + D], uT[:, 2 * n + q], bv[:], start=True, stop=True)
                last.then_inc(lowrank_filled, 1)
            for n in range(KD * KH // 4):
                if n < 2:
                    pe.wait_ge(w1_ready, 3 + n)
                else:
                    pe.wait_ge(w1_lo_done, n - 1)
                for q in range(4):
                    last = pe.transpose(ps_h[:, n % 2, P * q:P * q + P],
                                        wfc_sb[:, 4 * (n % 2) + q, P * (n // 2):P * (n // 2) + P], ident[:])
                last.then_inc(w1T_filled, 1)
            for c in range(KC):
                transpose_probs(0, c)
            pe.wait_ge(ident_bf_ready, 1)
            pe.wait_ge(tern2_ready, KD)
            t2 = tern2[:].rearrange("p k (q t) -> p k t q", t=KH)
            for n in range(2):
                pe.wait_ge(w1_lo_done, 3 + n)
                ps = ps_h[:, n].bitcast(BF16).rearrange("p (t d) -> p t d", t=4)
                for q in range(4):
                    for k in range(KD):
                        last = pe.transpose(ps[:, q, P * k:P * k + P], t2[:, k, 4 * n + q], ident_bf[:])
                last.then_inc(w2T_filled, 1)
            attend(0, 0, ffn=False)
            attend(0, 1, ffn=False)
            attend(0, 2, ffn=False)
            attend(0, 3, ffn=False)
            pe.wait_ge(xn_ready, 2)
            transpose_ln(xn, lambda k: ln1_fill(0, k))
            pe.wait_ge(w2T_ready, 1)
            pe.wait_ge(diag2_ready, 1)
            pe.wait_ge(consts_ready, 9)
            for k in range(KD):
                last = pe.matmul(ps_h[:, 0, P * k:P * k + P], ones[:], diag2[:, k], start=True, stop=True)
            last.then_inc(col_filled, 1)
            pe.wait_ge(x2n_ready, 2)
            transpose_ln(x2n, lambda k: ln2_fill(0, k, False))
            pe.wait_ge(w2T_ready, 2)
            pe.wait_ge(col_ready, 1)

            def both(i, last=False, head=False):
                f = i - 1
                pe.wait_ge(t_lo_done, ln1_fill(f, KD - 1) + 1)
                scores(i, 0)
                pe.wait_ge(t_lo_done, ln2_fill(f, KD - 1, False) + 1)
                hidden(f, 0, head)
                hidden(f, 1, head)
                scores(i, 1)
                hidden(f, 2)
                hidden(f, 3)
                scores(i, 2)
                hidden(f, 4)
                scores(i, 3)
                hidden(f, 5)
                hidden(f, 6)
                hidden(f, 7)
                transpose_probs(i, 0)
                transpose_probs(i, 1)
                project_out(f, 0)
                transpose_probs(i, 2)
                transpose_probs(i, 3)
                project_out(f, 1, head=head)
                transpose_probs(i, 4)
                attend(i, 0)
                project_out(f, 2)
                attend(i, 1)
                attend(i, 2)
                attend(i, 3)
                if not last:
                    pe.wait_ge(xn_ready, i + 2)
                    transpose_ln(xn, lambda k: ln1_fill(i, k))
                project_out(f, 3)
                pe.wait_ge(x2n_ready, 2 * i + 2)
                transpose_ln(x2n, lambda k: ln2_fill(i, k, last))

            both(1, head=True)
            with pe.Fori(2, NS - 1) as i:
                both(i)
            both(NS - 1, last=True)
            pe.wait_ge(t_lo_done, ln2_fill(NS - 1, KD - 1, True) + 1)
            for m in range(KH):
                hidden(NS - 1, m)
            for t in range(TT):
                project_out(NS - 1, t, attn=False)


_INS = ['x', 'ctx_768', 'mask_BxS2_bk0', 'g_xattn', 'g_ffn', 'L0_xattn_W_q', 'L0_xattn_W_k', 'L0_xattn_W_v',
        'L0_xattn_W_o', 'L0_xattn_b_o', 'L0_ffn_fast_b', 'L0_ffn_w_fc', 'L0_ffn_w_proj', 'L0_ffn_u', 'L0_ffn_v',
        'L0_ffn_gate']


def kernel(**inputs):
    import numpy as _np
    import concourse.bacc as _bacc
    from concourse import mybir as _mybir
    from concourse.bass_utils import run_bass_kernel_spmd as _run

    nc = _bacc.Bacc("TRN2", target_bir_lowering=False, num_devices=1)
    arrays, args = {}, []
    for name in _INS:
        a = _np.ascontiguousarray(inputs[name])
        if a.ndim == 0:
            a = a.reshape(1)
        arrays[f"in_{name}_dram"] = a
        args.append(nc.dram_tensor(f"in_{name}_dram", a.shape, _mybir.dt.from_np(a.dtype), kind="ExternalInput").ap())
    shape = inputs['x'].shape
    args.append(nc.dram_tensor("out_0_dram", shape, _mybir.dt.float32, kind="ExternalOutput").ap())
    block_kernel(nc, *args)
    r = _run(nc, [arrays], core_ids=[0])
    return r.results[0]["out_0_dram"]
```

```python
from contextlib import ExitStack

import concourse.bass as bass
from concourse import mybir

ALU = mybir.AluOpType
ACT = mybir.ActivationFunctionType
AX = mybir.AxisListType
F32 = mybir.dt.float32
F32R = mybir.dt.float32r
BF16 = mybir.dt.bfloat16
U8 = mybir.dt.uint8

P = 128
LN_EPS = 1e-5
SCALE_FLOOR = 1e-5
MASKED = -3.38e38


def block_kernel(nc, x, context, mask, g_xattn, g_ffn, w_q, w_k, w_v, w_o, b_o, fast_b, w_fc, w_proj,
                 u, v, gate, out):
    B, SEQ, D = x.shape
    J, C = context.shape[1:]
    INNER = w_q.shape[1]
    DH = 64
    HEADS = INNER // DH
    HID = w_fc.shape[0]
    RANK = u.shape[1]
    TT = 4
    TOK = TT * P
    NS = B * SEQ // TOK
    SPB = SEQ // TOK
    GROUPS = 4
    GP = P // GROUPS
    KD = D // P
    KI = INNER // P
    KH = HID // P
    HJ = HEADS * J
    HALF = HJ // 2
    BJ = B * J
    KC = (HJ + P - 1) // P
    CH = C // 2
    LASTROWS = HJ - (KC - 1) * P
    ATTN_SCALE = DH ** -0.5
    RING = 4

    ctx = ExitStack()
    with ctx:
        def sb(name, shape, dt=F32):
            return ctx.enter_context(nc.sbuf_tensor(name, shape, dt))

        def sem(name):
            return ctx.enter_context(nc.semaphore(name))

        with ExitStack() as passing:
            def early(name, shape, dt=F32):
                return passing.enter_context(nc.sbuf_tensor(name, shape, dt))

            wq_sb = early("wq_sb", [P, KD, INNER])
            wk_sb = early("wk_sb", [CH, 2, INNER])
            wv_sb = early("wv_sb", [CH, 2, INNER])
            wo_sb = early("wo_sb", [P, KI, D])
            wqT = early("wqT", [P, KI, D])
            kT = early("kT", [P, HEADS, BJ])
            vT = early("vT", [P, B, KI, 2 * P])
        pT_hi = sb("pT_hi", [P, KC, TOK], F32R)
        pT_lo = sb("pT_lo", [P, KC, TOK], F32R)
        x2nT_hi = sb("x2nT_hi", [P, KD, TOK], F32R)
        x2nT_lo = sb("x2nT_lo", [P, KD, TOK], F32R)
        x2n = sb("x2n", [P, TT, D])
        y_scaled = sb("y_scaled", [P, 2, D])
        with ExitStack() as passing:
            wfc_sb = early("wfc_sb", [P, KH, D])
            wproj_sb = early("wproj_sb", [P, KD, HID])
            below1 = early("below1", [P, KH, D], BF16)
            tern1 = early("tern1", [P, KH, D], BF16)
            u_groups = early("u_groups", [P, KH, P])
            below2 = early("below2", [P, KD, HID], BF16)
            above2 = early("above2", [P, HID], BF16)
            tern2 = early("tern2", [P, KD, HID], BF16)
        r2_hi = sb("r2_hi", [P, KH, TOK], F32R)
        r2_lo = sb("r2_lo", [P, KH, TOK], F32R)
        relu = sb("relu", [P, RING, TOK])
        square = sb("square", [P, RING, TOK])
        x_sb = sb("x_sb", [P, NS, TT, D])
        ctx_sb = sb("ctx_sb", [P, B, C])
        bo_row = sb("bo_row", [P, D])
        u_sb = sb("u_sb", [P, KH, RANK])
        v_sb = sb("v_sb", [RANK, D])
        fb_sb = sb("fb_sb", [RANK, RANK])
        gates = sb("gates", [P, 3])
        mask_row = sb("mask_row", [1, B, J], U8)
        ident = sb("ident", [P, P])
        ident_bf = sb("ident_bf", [P, P], BF16)
        ones = sb("ones", [P, P])
        ones_bf = sb("ones_bf", [P, P], BF16)
        head0_rows = sb("head0_rows", [P, P])
        minus_half = sb("minus_half", [P, TT])
        tanh_g = sb("tanh_g", [P, 2])
        ctxT = sb("ctxT", [CH, 2, B, J])
        a_hi = sb("a_hi", [P, KD, B, HJ], F32R)
        a_lo = sb("a_lo", [P, KD, B, HJ], F32R)
        vo_hi = sb("vo_hi", [P, B * KC, D], F32R)
        vo_lo = sb("vo_lo", [P, B * KC, D], F32R)
        mask_bias = sb("mask_bias", [P, B, HJ], BF16)
        scale1 = sb("scale1", [P, KH, 3])
        scale2 = sb("scale2", [P, KD, 3])
        inv_scale1 = sb("inv_scale1", [P, KH])
        select = sb("select", [RANK, GROUPS, GP])
        fbT = sb("fbT", [RANK, P])
        bvT = sb("bvT", [P, KD, P], F32R)
        uT = sb("uT", [P, KH, P], F32R)
        z = sb("z", [P, TOK], F32R)
        w1T = sb("w1T", [P, KD, KH, P], F32R)
        w2T = sb("w2T", [P, KH, D], F32R)
        diag2 = sb("diag2", [P, KD, P])
        col_scale = sb("col_scale", [P, D])
        xn = sb("xn", [P, TT, D])
        xnT_hi = sb("xnT_hi", [P, KD, TOK], F32R)
        xnT_lo = sb("xnT_lo", [P, KD, TOK], F32R)
        stats1 = sb("stats1", [P, TT, 6])
        moments1 = sb("moments1", [P, TT, 2])
        var1 = sb("var1", [P, TT])
        rstd1 = sb("rstd1", [P, TT])
        shift1 = sb("shift1", [P, TT])
        stats2 = sb("stats2", [P, TT, 6])
        moments2 = sb("moments2", [P, TT, 2])
        var2 = sb("var2", [P, TT])
        rstd2 = sb("rstd2", [P, TT])
        neg_max = sb("neg_max", [P, TT, HEADS])
        row_sum = sb("row_sum", [P, TT, HEADS])
        inv_sum = sb("inv_sum", [P, TT, HEADS])
        probs = sb("probs", [P, TT, HJ])

        ps_s = ctx.enter_context(nc.psum_tensor("ps_s", [P, 2, 512], F32))
        ps_t = ctx.enter_context(nc.psum_tensor("ps_t", [P, 2, 512], F32))
        ps_h = ctx.enter_context(nc.psum_tensor("ps_h", [P, 2, 512], F32))
        ps_o = ctx.enter_context(nc.psum_tensor("ps_o", [P, 2, 512], F32))
        banks = [ps_s[:, 0], ps_s[:, 1], ps_t[:, 0], ps_t[:, 1], ps_h[:, 0], ps_h[:, 1], ps_o[:, 0], ps_o[:, 1]]

        x_in = [sem(f"x_in{s}") for s in range(NS)]
        ctx_in, wq_in, wk_in, wv_in, wo_in, bo_in, mask_in = map(
            sem, ("ctx_in", "wq_in", "wk_in", "wv_in", "wo_in", "bo_in", "mask_in"))
        wfc_in, wproj_in, lowrank_in, gates_in, out_stored = map(
            sem, ("wfc_in", "wproj_in", "lowrank_in", "gates_in", "out_stored"))
        ident_ready, bo_row_zeroed, consts_ready, ident_bf_ready, tanh_ready, mask_ready = map(
            sem, ("ident_ready", "bo_row_zeroed", "consts_ready", "ident_bf_ready", "tanh_ready", "mask_ready"))
        ctxT_filled, ctxT_ready, wqT_filled, wqT_ready = map(sem, ("ctxT_filled", "ctxT_ready", "wqT_filled", "wqT_ready"))
        k_filled, k_ready, v_filled, v_ready = map(sem, ("k_filled", "k_ready", "v_filled", "v_ready"))
        a_filled, a_hi_done, a_lo_done, vo_filled, vo_hi_done, vo_lo_done = map(
            sem, ("a_filled", "a_hi_done", "a_lo_done", "vo_filled", "vo_hi_done", "vo_lo_done"))
        scale1_done, abs2_done, scale2_done, diag2_ready = map(sem, ("scale1_done", "abs2_done", "scale2_done", "diag2_ready"))
        below1_done, below2_done, above2_done, tern1_done, tern2_pool_half_done, tern2_dve_half_done = map(
            sem, ("below1_done", "below2_done", "above2_done", "tern1_done", "tern2_pool_half_done", "tern2_dve_half_done"))
        u_ready, uT_filled, uT_hi_done, uT_ready, select_ready, bank0_filled, fbT_ready = map(
            sem, ("u_ready", "uT_filled", "uT_hi_done", "uT_ready", "select_ready", "bank0_filled", "fbT_ready"))
        bvT_filled, bvT_hi_done, bvT_ready, w1T_filled, w1T_ready, w2T_filled, w2T_ready = map(
            sem, ("bvT_filled", "bvT_hi_done", "bvT_ready", "w1T_filled", "w1T_ready", "w2T_filled", "w2T_ready"))
        z_filled, z_hi_done, z_ready = map(sem, ("z_filled", "z_hi_done", "z_ready"))
        col_ready = sem("col_ready")
        ln1_stats, ln1_moments, ln1_var, ln1_rstd, shift1_done, xn_ready = map(
            sem, ("ln1_stats", "ln1_moments", "ln1_var", "ln1_rstd", "shift1_done", "xn_ready"))
        ln2_stats, ln2_moments, ln2_var, ln2_rstd, x2n_ready = map(
            sem, ("ln2_stats", "ln2_moments", "ln2_var", "ln2_rstd", "x2n_ready"))
        t_filled, t_hi_done, t_lo_done = map(sem, ("t_filled", "t_hi_done", "t_lo_done"))
        s_filled, max_done, shifted, exp_done, sum_done, inv_done, p_ready, p_last_ready = map(
            sem, ("s_filled", "max_done", "shifted", "exp_done", "sum_done", "inv_done", "p_ready", "p_last_ready"))
        o_filled, x2_done = map(sem, ("o_filled", "x2_done"))
        h_filled, relu_done, square_done, act_square_done, r2_hi_done, r2_lo_done = map(
            sem, ("h_filled", "relu_done", "square_done", "act_square_done", "r2_hi_done", "r2_lo_done"))
        dve_relu_done, square_even_done, square_odd_done = map(
            sem, ("dve_relu_done", "square_even_done", "square_odd_done"))
        y_filled, y_scaled_done, y_added, y_last_added = map(
            sem, ("y_filled", "y_scaled_done", "y_added", "y_last_added"))

        x_dram = x.rearrange("b (s p t) d -> (b s) p (t d)", p=P, t=TT)
        out_dram = out.rearrange("b (s p t) d -> (b s) p (t d)", p=P, t=TT)

        PER_S = KC + 2 * KD

        assert KC == TT + 1

        def probs_fill(i, c):
            return KD + PER_S * i + c

        def ln1_fill(i, k):
            return KD + PER_S * i + KC + k

        def ln2_fill(i, k, last):
            return KD + PER_S * i + KC + k + (0 if last else KD)

        def probs_views(c, to):
            if c < TT:
                return ps_t[:, c % 2].rearrange("p (k n) -> p k n", k=KC - 1), to[:, 0:KC - 1, P * c:P * c + P]
            return ps_t[0:LASTROWS, c % 2], to[0:LASTROWS, c]

        LN2_PARTS = (slice(0, TT - 1), slice(TT - 1, TT))

        A_BANKS = (7, 0, 1, 4, 5, 6, 7, 0)
        VO_BANKS = (2, 3, 4, 5, 4)
        SCORES0 = (ps_s, ps_o, ps_s, ps_o)

        POOL_SQUARES = (0, 1, 2, 4, 5, 6, 7)
        ACT_SQUARES = (3,)

        def squares_before(f, m):
            return len(POOL_SQUARES) * f + POOL_SQUARES.index(m)

        def batch(i):
            return i // SPB

        ATTN_OUT = (ps_s[:, 0], ps_s[:, 1], ps_o[:, 1], ps_s[:, 0])
        FFN_OUT = (ps_o[:, 0], ps_s[:, 1], ps_o[:, 0], ps_o[:, 1])
        FIRST_OUT = (ps_o[:, 0], ps_o[:, 1], ps_o[:, 0], ps_o[:, 1])
        FIRST_Z = ps_o[:, 0]
        LAST_Z = ps_s[:, 0]
        LAST_H = (ps_h[:, 0], ps_h[:, 1], ps_s[:, 1], ps_s[:, 0], ps_t[:, 0], ps_t[:, 1], ps_h[:, 0], ps_h[:, 1])
        LAST_DVE_RELUS = (1, 4)

        def wait_last_relu(engine, m):
            if m in LAST_DVE_RELUS:
                engine.wait_ge(dve_relu_done, LAST_DVE_RELUS.index(m) + 1)
            else:
                before = sum(n < m for n in LAST_DVE_RELUS)
                engine.wait_ge(relu_done, KH * (NS - 1) + m - before + 1)

        LAST_Y = (ps_o[:, 0], ps_o[:, 1], ps_s[:, 1], ps_s[:, 0])

        block = ctx.enter_context(nc.Block())

        @block.sync
        def _(sp):
            sp.dma_start(ctx_sb[0:J], context.rearrange("b j c -> j b c")).then_inc(ctx_in, 16)
            sp.dma_start(wk_sb[:], w_k.rearrange("(k p) n -> p k n", p=CH)).then_inc(wk_in, 16)
            sp.dma_start(wq_sb[:], w_q.rearrange("(k p) n -> p k n", p=P)).then_inc(wq_in, 16)
            sp.dma_start(x_sb[:, 0].rearrange("p t d -> p (t d)"), x_dram[0]).then_inc(x_in[0], 16)
            sp.dma_start(wv_sb[:], w_v.rearrange("(k p) n -> p k n", p=CH)).then_inc(wv_in, 16)
            sp.dma_start(mask_row[:], mask.rearrange("(a b) j -> a b j", a=1)).then_inc(mask_in, 16)
            sp.dma_start(wfc_sb[:], w_fc.rearrange("(p t) d -> p t d", t=KH)).then_inc(wfc_in, 16)
            for n, g in enumerate((g_xattn, g_ffn, gate)):
                sp.dma_start(gates[:, n:n + 1],
                             g.rearrange("(a b) -> a b", a=1).to_broadcast([P, 1])).then_inc(gates_in, 16)
            sp.wait_ge(bo_row_zeroed, 1)
            sp.dma_start(bo_row[0:1, :], b_o.rearrange("(a d) -> a d", a=1)).then_inc(bo_in, 16)
            sp.dma_start(wo_sb[:], w_o.rearrange("(k p) n -> p k n", p=P)).then_inc(wo_in, 16)
            sp.dma_start(u_sb[:], u.rearrange("(p t) r -> p t r", t=KH)).then_inc(lowrank_in, 16)
            sp.dma_start(v_sb[:], v).then_inc(lowrank_in, 16)
            sp.dma_start(fb_sb[:], fast_b).then_inc(lowrank_in, 16)
            sp.dma_start(wproj_sb[:], w_proj.rearrange("(k p) n -> p k n", p=P)).then_inc(wproj_in, 16)
            for s in range(1, NS):
                sp.dma_start(x_sb[:, s].rearrange("p t d -> p (t d)"), x_dram[s]).then_inc(x_in[s], 16)
            with sp.Fori(0, NS - 1) as s:
                sp.wait_ge(y_added, TT * s + TT)
                sp.dma_start(out_dram[s], x_sb[:, s].rearrange("p t d -> p (t d)")).then_inc(out_stored, 16)
            for t in range(TT):
                sp.wait_ge(y_last_added, t + 1)
                sp.dma_start(out_dram[NS - 1, :, t * D:(t + 1) * D], x_sb[:, NS - 1, t]).then_inc(out_stored, 16)
            sp.wait_ge(out_stored, 16 * (NS - 1 + TT))

        @block.gpsimd
        def _(pool):
            pool.memset(ident[:], 0.0).then_inc(consts_ready, 1)
            pool.wait_ge(consts_ready, 1)
            pool.affine_select(out=ident[:], in_=ident[:], compare_op=ALU.not_equal, fill=1.0, base=0,
                               pattern=[[-1, P]], channel_multiplier=1).then_inc(ident_ready, 1)
            pool.memset(bo_row[:], 0.0).then_inc(bo_row_zeroed, 1)
            pool.memset(minus_half[:], -0.5).then_inc(consts_ready, 1)
            pool.memset(kT[:], 0.0).then_inc(consts_ready, 1)
            pool.memset(mask_bias[:], 0.0).then_inc(consts_ready, 1)
            pool.memset(ones_bf[:], 1.0).then_inc(consts_ready, 1)
            pool.memset(head0_rows[:], 0.0).then_inc(consts_ready, 1)
            pool.wait_ge(consts_ready, 6)
            pool.memset(head0_rows[0:1, 0:J], 1.0).then_inc(consts_ready, 1)
            pool.memset(vT[:], 0.0).then_inc(consts_ready, 1)
            pool.memset(ones[:], 1.0).then_inc(consts_ready, 1)
            pool.memset(u_groups[:], 0.0).then_inc(consts_ready, 1)

            def rstd1_step(i):
                pool.wait_ge(ln1_var, i + 1)
                pool.tensor_tensor(rstd1[:], var1[:], minus_half[:], ALU.pow).then_inc(ln1_rstd, 1)

            def rstd2_step(i, part):
                pool.wait_ge(ln2_var, 2 * i + part + 1)
                tiles = LN2_PARTS[part]
                pool.tensor_tensor(rstd2[:, tiles], var2[:, tiles], minus_half[:, tiles], ALU.pow).then_inc(ln2_rstd, 1)

            def normalise(i, t):
                pool.wait_ge(inv_done, TT * i + t + 1)
                p3 = probs[:, t].rearrange("p (h j) -> p h j", h=HEADS)
                pool.tensor_tensor(p3, p3, inv_sum[:, t].unsqueeze(2).to_broadcast([P, HEADS, J]),
                                   ALU.mult).then_inc(p_ready, 1)

            def square_step(f, m, head=False):
                pool.wait_ge(relu_done, KH * f + m + 1)
                if not (head and m < RING):
                    pool.wait_ge(r2_lo_done, KH * f + m - RING + 1)
                pool.tensor_tensor(square[:, m % RING], relu[:, m % RING], relu[:, m % RING],
                                   ALU.mult).then_inc(square_done, 1)

            def add_step(f, t):
                pool.wait_ge(y_scaled_done, TT * f + t + 1)
                pool.tensor_tensor(x_sb[:, f, t], y_scaled[:, t % 2], x_sb[:, f, t], ALU.add).then_inc(y_added, 1)

            rstd1_step(0)
            pool.wait_ge(mask_in, 16)
            pool.wait_ge(consts_ready, 4)
            for h in range(HEADS):
                last = pool.tensor_scalar(mask_bias[0:1, :, h * J:(h + 1) * J], mask_row[:], -1.0, -MASKED,
                                          ALU.add, ALU.mult)
            last.then_inc(mask_ready, 1)

            def below1_step(t):
                pool.wait_ge(scale1_done, 3)
                pool.tensor_scalar(below1[:, t], wfc_sb[:, t], scale1[:, t, 2:3], None, ALU.is_lt).then_inc(below1_done, 1)

            def below2_step(k):
                pool.wait_ge(scale2_done, 2)
                pool.tensor_scalar(below2[:, k], wproj_sb[:, k], scale2[:, k, 2:3], None, ALU.is_lt).then_inc(below2_done, 1)

            def ternary2_half():
                pool.tensor_scalar(above2[:], wproj_sb[:, 0], scale2[:, 0, 1:2], None, ALU.is_gt).then_inc(above2_done, 1)
                pool.wait_ge(below2_done, 1)
                pool.wait_ge(above2_done, 1)
                pool.tensor_tensor(tern2[:, 0], above2[:], below2[:, 0], ALU.subtract).then_inc(tern2_pool_half_done, 1)

            for t in range(5):
                below1_step(t)
            normalise(0, 0)
            for t in range(5, KH):
                below1_step(t)
            normalise(0, 1)
            below2_step(0)
            normalise(0, 2)
            below2_step(1)
            rstd1_step(1)
            ternary2_half()
            rstd2_step(0, 0)
            rstd2_step(0, 1)

            def both(i, last=False, head=False):
                f = i - 1
                normalise(i, 0)
                square_step(f, 0, head)
                square_step(f, 1, head)
                normalise(i, 1)
                square_step(f, 2, head)
                normalise(i, 2)
                square_step(f, 4)
                square_step(f, 5)
                square_step(f, 6)
                if not last:
                    rstd1_step(i + 1)
                square_step(f, 7)
                add_step(f, 0)
                rstd2_step(i, 0)
                rstd2_step(i, 1)
                for t in range(1, TT):
                    add_step(f, t)

            both(1, head=True)
            with pool.Fori(2, NS - 1) as i:
                both(i)
            both(NS - 1, last=True)
            for m in range(0, KH, 2):
                wait_last_relu(pool, m)
                pool.wait_ge(r2_lo_done, KH * (NS - 1) + m - RING + 1)
                pool.tensor_tensor(square[:, m % RING], relu[:, m % RING], relu[:, m % RING],
                                   ALU.mult).then_inc(square_even_done, 1)

        @block.scalar
        def _(act):
            def split_hi(f, k, to):
                act.wait_ge(t_filled, f + 1)
                act.activation(to, k, ACT.Identity).then_inc(t_hi_done, 1)

            def split_ln(fill, to):
                for k in range(KD):
                    split_hi(fill(k), ps_t[:, (1 + k) % 2], to[:, k])

            def split_probs(i, c):
                split_hi(probs_fill(i, c), *probs_views(c, pT_hi))

            def exp_heads(t):
                act.wait_ge(max_done, t + 1)
                for h in range(HEADS):
                    half, g = divmod(h, HEADS // 2)
                    last = act.activation(probs[:, t, h * J:(h + 1) * J], SCORES0[t][:, half, g * J:(g + 1) * J], ACT.Exp,
                                          bias=neg_max[:, t, h:h + 1], accum_out=row_sum[:, t, h:h + 1])
                last.then_inc(exp_done, 1)

            def exp_step(i, t):
                act.wait_ge(shifted, TT * (i - 1) + t + 1)
                act.activation(probs[:, t], probs[:, t], ACT.Exp).then_inc(exp_done, 1)

            def relu_step(f, m, head=False):
                act.wait_ge(h_filled, KH * f + m + 1)
                if m - RING in POOL_SQUARES:
                    act.wait_ge(square_done, squares_before(f, m - RING) + 1)
                elif m < RING and m + RING in POOL_SQUARES and not head:
                    act.wait_ge(square_done, squares_before(f - 1, m + RING) + 1)
                act.activation(relu[:, m % RING], ps_h[:, m % 2], ACT.Relu, scale=scale1[:, m, 0:1]).then_inc(relu_done, 1)

            def normalise_xn(i):
                act.wait_ge(shift1_done, i)
                for t in range(TT):
                    last = act.activation(xn[:, t], x_sb[:, i, t], ACT.Identity, bias=shift1[:, t:t + 1],
                                          scale=rstd1[:, t:t + 1])
                last.then_inc(xn_ready, 1)

            def z_hi(f, to=ps_h[:, 1]):
                act.wait_ge(z_filled, f + 1)
                act.activation(z[:], to[:], ACT.Identity).then_inc(z_hi_done, 1)

            def square_full(f, m, head=False):
                act.wait_ge(relu_done, KH * f + m + 1)
                if not (head and m < RING):
                    act.wait_ge(r2_lo_done, KH * f + m - RING + 1)
                act.activation(square[:, m % RING], relu[:, m % RING], ACT.Square).then_inc(act_square_done, 1)

            def square_hi(f, m):
                act.wait_ge(relu_done, KH * f + m + 1)
                act.activation(r2_hi[:, m], relu[:, m % RING], ACT.Square).then_inc(r2_hi_done, 1)

            act.wait_ge(consts_ready, 2)
            act.activation(tanh_g[:, 0:1], minus_half[:, 0:1], ACT.Tanh)
            act.wait_ge(ctxT_filled, 1)
            act.activation(ctxT[:], banks[0][0:CH].rearrange("p (k b j) -> p k b j", k=2, b=B)[:, :, :, 0:J],
                           ACT.Identity).then_inc(ctxT_ready, 1)
            act.wait_ge(consts_ready, 3)

            def key_step(n):
                act.wait_ge(k_filled, n + 1)
                ps = banks[5 + n].rearrange("p (c n) -> p c n", c=2)[:, :, 0:BJ]
                to = kT[:, 4 * n:4 * n + 4].rearrange("p (c e) n -> p c e n", e=2)
                for e in range(2):
                    rows = slice(DH * e, DH * e + DH)
                    last = act.activation(to[rows, :, e], ps[rows], ACT.Identity, scale=ATTN_SCALE)
                last.then_inc(k_ready, 1)

            key_step(0)
            for n in range(2):
                act.wait_ge(wqT_filled, n + 1)
                act.activation(wqT[:, 2 * n:2 * n + 2], banks[(1, 4)[n]].rearrange("p (c d) -> p c d", c=2),
                               ACT.Identity).then_inc(wqT_ready, 1)
            key_step(1)
            for n in range(KD * KI):
                c, m = divmod(n, KD)
                act.wait_ge(a_filled, n + 1)
                act.activation(a_hi[:, m, :, 2 * c * J:2 * (c + 1) * J].rearrange("p b (h j) -> p h b j", h=2),
                               banks[A_BANKS[n]][:, 0:2 * BJ].rearrange("p (h b j) -> p h b j", h=2, b=B),
                               ACT.Identity).then_inc(a_hi_done, 1)

            split_ln(lambda k: k, xnT_hi)
            act.wait_ge(consts_ready, 8)
            for n in range(2):
                act.wait_ge(v_filled, n + 1)
                for c in (2 * n, 2 * n + 1):
                    for e in range(2):
                        rows, at = slice(DH * e, DH * e + DH), (2 * c + e) * J - P * c
                        last = act.activation(vT[rows, :, c, at:at + J],
                                              banks[4 + n][rows, 256 * (c % 2):256 * (c % 2) + BJ].rearrange("p (b j) -> p b j", b=B),
                                              ACT.Identity)
                last.then_inc(v_ready, 1)
            act.wait_ge(gates_in, 48)
            act.activation(tanh_g[:], gates[:, 0:2], ACT.Tanh).then_inc(tanh_ready, 1)
            act.wait_ge(wproj_in, 16)
            for k in range(KD):
                act.activation(tern2[:, k], wproj_sb[:, k], ACT.Abs, accum_out=scale2[:, k, 0:1]).then_inc(abs2_done, 1)

            def vo_step(n):
                act.wait_ge(vo_filled, n + 1)
                act.activation(vo_hi[:, 2 * n:2 * n + 2], banks[VO_BANKS[n]].rearrange("p (k d) -> p k d", k=2),
                               ACT.Identity, scale=tanh_g[:, 0:1]).then_inc(vo_hi_done, 1)

            exp_heads(0)
            act.wait_ge(tanh_ready, 1)
            vo_step(0)
            exp_heads(1)
            vo_step(1)
            exp_heads(2)
            vo_step(2)
            exp_heads(3)
            act.wait_ge(bank0_filled, 1)
            act.activation(fbT[:], banks[0][0:RANK, 0:P], ACT.Identity).then_inc(fbT_ready, 1)
            vo_step(3)
            vo_step(4)
            split_probs(0, 0)
            act.activation(col_scale[:], banks[0][:, P:P + D], ACT.Identity).then_inc(col_ready, 1)
            split_probs(0, 1)
            act.wait_ge(bvT_filled, 1)
            act.activation(bvT[:], banks[1][:, 0:KD * P].rearrange("p (k n) -> p k n", k=KD),
                           ACT.Identity).then_inc(bvT_hi_done, 1)

            def w1_step(k):
                act.wait_ge(w1T_filled, k + 1)
                act.activation(w1T[:, k], ps_o[:, k].bitcast(BF16).rearrange("p (t n) -> p t n", t=KH),
                               ACT.Identity).then_inc(w1T_ready, 1)

            def uT_step(n):
                act.wait_ge(uT_filled, n + 1)
                act.activation(uT[:, 4 * n:4 * n + 4], banks[4 + n].rearrange("p (t n) -> p t n", t=4),
                               ACT.Identity).then_inc(uT_hi_done, 1)

            w1_step(0)
            split_probs(0, 2)
            split_probs(0, 3)
            uT_step(0)
            split_probs(0, 4)
            w1_step(1)
            uT_step(1)
            normalise_xn(1)
            split_ln(lambda k: ln1_fill(0, k), xnT_hi)

            def w2_step(n):
                act.wait_ge(w2T_filled, n + 1)
                act.activation(w2T[:, 4 * n:4 * n + 4], ps_o[:, n].bitcast(BF16).rearrange("p (t d) -> p t d", t=4),
                               ACT.Identity).then_inc(w2T_ready, 1)

            def both(i, last=False, head=False):
                f = i - 1
                if head:
                    split_ln(lambda k: ln2_fill(f, k, False), x2nT_hi)
                    exp_step(i, 0)
                    w2_step(0)
                    w2_step(1)
                    z_hi(f, FIRST_Z)
                    exp_step(i, 1)
                else:
                    z_hi(f)
                    exp_step(i, 0)
                relu_step(f, 0, head)
                square_hi(f, 0)
                if not head:
                    exp_step(i, 1)
                relu_step(f, 1, head)
                split_probs(i, 0)
                square_hi(f, 1)
                relu_step(f, 2, head)
                exp_step(i, 2)
                square_hi(f, 2)
                relu_step(f, 3, head)
                square_hi(f, 3)
                square_full(f, 3, head)
                split_probs(i, 1)
                relu_step(f, 4)
                exp_step(i, 3)
                if head:
                    relu_step(f, 5)
                    square_hi(f, 4)
                else:
                    square_hi(f, 4)
                    relu_step(f, 5)
                split_probs(i, 2)
                relu_step(f, 6)
                square_hi(f, 5)
                split_probs(i, 3)
                split_probs(i, 4)
                square_hi(f, 6)
                relu_step(f, 7)
                square_hi(f, 7)
                if not last:
                    normalise_xn(i + 1)
                    split_ln(lambda k: ln1_fill(i, k), xnT_hi)
                split_ln(lambda k: ln2_fill(i, k, last), x2nT_hi)

            both(1, head=True)
            with act.Fori(2, NS - 1) as i:
                both(i)
            both(NS - 1, last=True)
            z_hi(NS - 1, LAST_Z)
            for m in range(KH):
                if m not in LAST_DVE_RELUS:
                    act.wait_ge(h_filled, KH * (NS - 1) + m + 1)
                    act.wait_ge(r2_lo_done, KH * (NS - 1) + m - RING + 1)
                    act.activation(relu[:, m % RING], LAST_H[m], ACT.Relu, scale=scale1[:, m, 0:1]).then_inc(relu_done, 1)
                wait_last_relu(act, m)
                act.activation(r2_hi[:, m], relu[:, m % RING], ACT.Square).then_inc(r2_hi_done, 1)

        @block.vector
        def _(dve):
            def settled():
                dve.wait_ge(ident_ready, 1)

            def ln1_stats_step(i, t):
                settled()
                dve.bn_stats(stats1[:, t], x_sb[:, i, t]).then_inc(ln1_stats, 1)

            def ln1_moments_step(i):
                dve.wait_ge(ln1_stats, TT * i + TT)
                settled()
                for t in range(TT):
                    last = dve.bn_aggr(moments1[:, t], stats1[:, t])
                last.then_inc(ln1_moments, 1)
                dve.wait_ge(ln1_moments, i + 1)
                dve.tensor_scalar(var1[:], moments1[:, :, 1], LN_EPS, None, ALU.add).then_inc(ln1_var, 1)

            def shift1_step(i):
                dve.wait_ge(ln1_rstd, i + 1)
                settled()
                dve.scalar_tensor_tensor(out=shift1[:], in0=moments1[:, :, 0], scalar=-1.0, in1=rstd1[:],
                                         op0=ALU.mult, op1=ALU.mult).then_inc(shift1_done, 1)

            def ln1_normalise():
                dve.wait_ge(ln1_rstd, 1)
                for t in range(TT):
                    last = dve.tensor_scalar(xn[:, t], x_sb[:, 0, t], moments1[:, t, 0:1], rstd1[:, t:t + 1],
                                             ALU.subtract, ALU.mult)
                last.then_inc(xn_ready, 1)

            def residual_add(i, t, at=ATTN_OUT):
                dve.wait_ge(o_filled, TT * i + t + 1)
                dve.tensor_tensor(x_sb[:, i, t], at[t][:, 0:D], x_sb[:, i, t], ALU.add).then_inc(x2_done, 1)

            def ln2_stats_step(i, t):
                dve.wait_ge(x2_done, TT * i + t + 1)
                settled()
                dve.bn_stats(stats2[:, t], x_sb[:, i, t]).then_inc(ln2_stats, 1)

            def ln2_moments_step(i, t):
                dve.wait_ge(ln2_stats, TT * i + t + 1)
                settled()
                dve.bn_aggr(moments2[:, t], stats2[:, t]).then_inc(ln2_moments, 1)

            def residual(i, t, at=ATTN_OUT):
                residual_add(i, t, at)
                ln2_stats_step(i, t)
                ln2_moments_step(i, t)

            def ln2_var_step(i, part):
                tiles = LN2_PARTS[part]
                dve.wait_ge(ln2_moments, TT * i + tiles.stop)
                dve.tensor_scalar(var2[:, tiles], moments2[:, tiles, 1], LN_EPS, None, ALU.add).then_inc(ln2_var, 1)

            def ln2_normalise(i, part):
                dve.wait_ge(ln2_rstd, 2 * i + part + 1)
                for t in range(LN2_PARTS[part].start, LN2_PARTS[part].stop):
                    last = dve.tensor_scalar(x2n[:, t], x_sb[:, i, t], moments2[:, t, 0:1], rstd2[:, t:t + 1],
                                             ALU.subtract, ALU.mult)
                last.then_inc(x2n_ready, 1)

            def split_lo(f, ps, hi, lo):
                dve.wait_ge(t_hi_done, f + 1)
                dve.tensor_tensor(lo, ps, hi.bitcast(F32), ALU.subtract).then_inc(t_lo_done, 1)

            def split_probs(i, c):
                ps, hi = probs_views(c, pT_hi)
                split_lo(probs_fill(i, c), ps, hi, probs_views(c, pT_lo)[1])

            def split_xn(i, k):
                split_lo(ln1_fill(i, k), ps_t[:, (1 + k) % 2], xnT_hi[:, k], xnT_lo[:, k])

            def split_x2n(i, k, last=False):
                split_lo(ln2_fill(i, k, last), ps_t[:, (1 + k) % 2], x2nT_hi[:, k], x2nT_lo[:, k])

            heads4 = ps_s[:, :, 0:HALF].rearrange("p b (h j) -> p b h j", h=HEADS // 2)

            def shift_step(i, t):
                dve.wait_ge(s_filled, TT * i + t + 1)
                dve.tensor_reduce(neg_max[:, t], heads4, AX.X, ALU.max, negate=True).then_inc(max_done, 1)
                dve.wait_ge(max_done, TT * i + t + 1)
                shift = neg_max[:, t].rearrange("p (b h) -> p b h", b=2).unsqueeze(3).to_broadcast([P, 2, HEADS // 2, J])
                dve.tensor_tensor(probs[:, t].rearrange("p (b h j) -> p b h j", b=2, h=HEADS // 2), heads4, shift,
                                  ALU.add).then_inc(shifted, 1)

            def sum_step(i, t):
                dve.wait_ge(exp_done, TT * i + t + 1)
                dve.tensor_reduce(row_sum[:, t], probs[:, t].rearrange("p (h j) -> p h j", h=HEADS), AX.X,
                                  ALU.add).then_inc(sum_done, 1)
                dve.wait_ge(sum_done, TT * (i - 1) + t + 1)
                dve.reciprocal(inv_sum[:, t], row_sum[:, t]).then_inc(inv_done, 1)

            def normalise_last(i):
                dve.wait_ge(inv_done, TT * i + TT)
                p3 = probs[:, TT - 1].rearrange("p (h j) -> p h j", h=HEADS)
                dve.tensor_tensor(p3, p3, inv_sum[:, TT - 1].unsqueeze(2).to_broadcast([P, HEADS, J]),
                                  ALU.mult).then_inc(p_last_ready, 1)

            def z_lo(f, to=ps_h[:, 1]):
                dve.wait_ge(z_hi_done, f + 1)
                rows = slice(2 * GP, 3 * GP)
                dve.tensor_tensor(z[rows], to[rows], z[rows].bitcast(F32), ALU.subtract).then_inc(z_ready, 1)

            def split_square(f, m):
                if m in POOL_SQUARES:
                    dve.wait_ge(square_done, squares_before(f, m) + 1)
                else:
                    dve.wait_ge(act_square_done, len(ACT_SQUARES) * f + ACT_SQUARES.index(m) + 1)
                dve.wait_ge(r2_hi_done, KH * f + m + 1)
                dve.tensor_tensor(r2_lo[:, m], square[:, m % RING], r2_hi[:, m].bitcast(F32),
                                  ALU.subtract).then_inc(r2_lo_done, 1)

            def y_step(f, t, head=False):
                dve.wait_ge(y_filled, TT * f + t + 1)
                if not (head and t < 2):
                    dve.wait_ge(y_added, TT * f + t - 1)
                dve.tensor_tensor(y_scaled[:, t % 2], FFN_OUT[t][:, 0:D], col_scale[:],
                                  ALU.mult).then_inc(y_scaled_done, 1)

            def a_split(n):
                c, m = divmod(n, KD)
                dve.wait_ge(a_hi_done, n + 1)
                view = [a[:, m, :, 2 * c * J:2 * (c + 1) * J].rearrange("p b (h j) -> p h b j", h=2) for a in (a_lo, a_hi)]
                dve.tensor_tensor(view[0], banks[A_BANKS[n]][:, 0:2 * BJ].rearrange("p (h b j) -> p h b j", h=2, b=B),
                                  view[1].bitcast(F32), ALU.subtract).then_inc(a_lo_done, 1)

            dve.wait_ge(x_in[0], 16)
            for t in range(TT):
                ln1_stats_step(0, t)
            ln1_moments_step(0)
            for n in range(3):
                a_split(n)
            ln1_normalise()
            for n in range(3, KD * KI):
                a_split(n)
            dve.tensor_copy(ident_bf[:], ident[:]).then_inc(ident_bf_ready, 1)
            dve.tensor_copy(select[:], ident[0:RANK, 0:GP].unsqueeze(1).to_broadcast([RANK, GROUPS, GP])).then_inc(select_ready, 1)
            for k in range(KD):
                split_lo(k, ps_t[:, (1 + k) % 2], xnT_hi[:, k], xnT_lo[:, k])
            dve.wait_ge(wfc_in, 16)
            dve.tensor_reduce(scale1[:, :, 0], wfc_sb[:], AX.X, ALU.add, apply_absolute_value=True).then_inc(scale1_done, 1)
            dve.wait_ge(scale1_done, 1)
            dve.tensor_scalar(scale1[:, :, 0], scale1[:, :, 0], 1.0 / D, SCALE_FLOOR, ALU.mult, ALU.max).then_inc(scale1_done, 1)
            dve.wait_ge(scale1_done, 2)
            dve.tensor_scalar(scale1[:, :, 1], scale1[:, :, 0], 0.5, None, ALU.mult)
            dve.tensor_scalar(scale1[:, :, 2], scale1[:, :, 0], -0.5, None, ALU.mult).then_inc(scale1_done, 1)

            def ternary1(t):
                dve.wait_ge(below1_done, t + 1)
                dve.scalar_tensor_tensor(out=tern1[:, t], in0=wfc_sb[:, t], scalar=scale1[:, t, 1:2], in1=below1[:, t],
                                         op0=ALU.is_gt, op1=ALU.subtract).then_inc(tern1_done, 1)

            def max_step(t):
                dve.wait_ge(s_filled, t + 1)
                heads = SCORES0[t][:, :, 0:HALF].rearrange("p b (h j) -> p b h j", h=HEADS // 2)
                dve.tensor_reduce(neg_max[:, t], heads, AX.X, ALU.max, negate=True).then_inc(max_done, 1)

            def inv_step(t):
                dve.wait_ge(exp_done, t + 1)
                dve.reciprocal(inv_sum[:, t], row_sum[:, t]).then_inc(inv_done, 1)

            def vo_step(n):
                dve.wait_ge(vo_hi_done, n + 1)
                dve.scalar_tensor_tensor(out=vo_lo[:, 2 * n:2 * n + 2],
                                         in0=banks[VO_BANKS[n]].rearrange("p (k d) -> p k d", k=2),
                                         scalar=tanh_g[:, 0:1], in1=vo_hi[:, 2 * n:2 * n + 2].bitcast(F32),
                                         op0=ALU.mult, op1=ALU.subtract).then_inc(vo_lo_done, 1)

            max_step(0)
            dve.wait_ge(abs2_done, KD)
            dve.tensor_scalar(scale2[:, :, 0], scale2[:, :, 0], 1.0 / HID, SCALE_FLOOR, ALU.mult, ALU.max).then_inc(scale2_done, 1)
            dve.wait_ge(scale2_done, 1)
            dve.tensor_scalar(scale2[:, :, 1], scale2[:, :, 0], 0.5, None, ALU.mult)
            dve.tensor_scalar(scale2[:, :, 2], scale2[:, :, 0], -0.5, None, ALU.mult).then_inc(scale2_done, 1)
            dve.reciprocal(inv_scale1[:], scale1[:, :, 0]).then_inc(scale1_done, 1)
            dve.wait_ge(scale1_done, 4)
            dve.wait_ge(lowrank_in, 48)
            dve.wait_ge(gates_in, 48)
            dve.wait_ge(consts_ready, 10)
            for g in range(GROUPS):
                last = dve.scalar_tensor_tensor(out=u_groups[:, :, GP * g:GP * g + RANK], in0=u_sb[:], scalar=gates[:, 2:3],
                                                in1=inv_scale1[:].unsqueeze(2).to_broadcast([P, KH, RANK]),
                                                op0=ALU.mult, op1=ALU.mult)
            last.then_inc(u_ready, 1)
            for k in range(KD):
                last = dve.tensor_scalar(diag2[:, k], ident[:], scale2[:, k, 0:1], tanh_g[:, 1:2], ALU.mult, ALU.mult)
            last.then_inc(diag2_ready, 1)
            max_step(1)
            inv_step(0)
            dve.wait_ge(tanh_ready, 1)
            vo_step(0)
            for t in range(4):
                ternary1(t)
            max_step(2)
            inv_step(1)
            vo_step(1)
            for t in range(4, KH):
                ternary1(t)
            max_step(3)
            inv_step(2)
            vo_step(2)
            for s in range(1, NS):
                dve.wait_ge(x_in[s], 16)
            for t in range(TT):
                ln1_stats_step(1, t)
            ln1_moments_step(1)
            inv_step(3)
            normalise_last(0)
            vo_step(3)
            vo_step(4)
            split_probs(0, 0)
            split_probs(0, 1)
            dve.wait_ge(bvT_hi_done, 1)
            cols = slice(3 * GP, 4 * GP)
            dve.tensor_tensor(bvT[:, :, cols], banks[1][:, 0:KD * P].rearrange("p (k n) -> p k n", k=KD)[:, :, cols],
                              bvT[:, :, cols].bitcast(F32), ALU.subtract).then_inc(bvT_ready, 1)
            split_probs(0, 2)
            split_probs(0, 3)
            shift1_step(1)
            split_probs(0, 4)
            dve.wait_ge(below2_done, KD)
            dve.scalar_tensor_tensor(out=tern2[:, 1], in0=wproj_sb[:, 1], scalar=scale2[:, 1, 1:2], in1=below2[:, 1],
                                     op0=ALU.is_gt, op1=ALU.subtract).then_inc(tern2_dve_half_done, 1)

            def uT_split(n):
                dve.wait_ge(uT_hi_done, n + 1)
                rows = slice(GP, 2 * GP)
                dve.tensor_tensor(uT[rows, 4 * n:4 * n + 4], banks[4 + n][rows].rearrange("p (t n) -> p t n", t=4),
                                  uT[rows, 4 * n:4 * n + 4].bitcast(F32), ALU.subtract).then_inc(uT_ready, 1)

            residual_add(0, 0, FIRST_OUT)
            uT_split(0)
            ln2_stats_step(0, 0)
            residual_add(0, 1, FIRST_OUT)
            ln2_moments_step(0, 0)
            ln2_stats_step(0, 1)
            residual_add(0, 2, FIRST_OUT)
            ln2_moments_step(0, 1)
            ln2_stats_step(0, 2)
            split_xn(0, 0)
            ln2_moments_step(0, 2)
            split_xn(0, 1)
            ln2_var_step(0, 0)
            residual(0, 3, FIRST_OUT)
            ln2_var_step(0, 1)
            ln2_normalise(0, 0)
            ln2_normalise(0, 1)

            def both(i, last=False, head=False):
                f = i - 1
                shift_step(i, 0)
                if head:
                    uT_split(1)
                    split_x2n(f, 0)
                    split_x2n(f, 1)
                    shift_step(i, 1)
                    z_lo(f, FIRST_Z)
                    sum_step(i, 0)
                    sum_step(i, 1)
                    ln1_stats_step(i + 1, 0)
                    ln1_stats_step(i + 1, 1)
                    shift_step(i, 2)
                    split_square(f, 0)
                else:
                    z_lo(f)
                    if not last:
                        ln1_stats_step(i + 1, 0)
                    sum_step(i, 0)
                    shift_step(i, 1)
                    if not last:
                        ln1_stats_step(i + 1, 1)
                        ln1_stats_step(i + 1, 2)
                    split_square(f, 0)
                    sum_step(i, 1)
                    shift_step(i, 2)
                split_probs(i, 0)
                split_square(f, 1)
                sum_step(i, 2)
                if not last and not head:
                    ln1_stats_step(i + 1, 3)
                shift_step(i, 3)
                split_probs(i, 1)
                if head:
                    ln1_stats_step(i + 1, 2)
                split_square(f, 2)
                sum_step(i, 3)
                normalise_last(i)
                split_probs(i, 2)
                if not last and not head:
                    ln1_moments_step(i + 1)
                split_square(f, 3)
                split_probs(i, 3)
                split_probs(i, 4)
                if head:
                    ln1_stats_step(i + 1, 3)
                    ln1_moments_step(i + 1)
                split_square(f, 4)
                split_square(f, 5)
                if head:
                    shift1_step(i + 1)
                residual_add(i, 0)
                split_square(f, 6)
                ln2_stats_step(i, 0)
                if not last and not head:
                    shift1_step(i + 1)
                ln2_moments_step(i, 0)
                residual_add(i, 1)
                split_square(f, 7)
                ln2_stats_step(i, 1)
                ln2_moments_step(i, 1)
                residual_add(i, 2)
                y_step(f, 0, head=head)
                ln2_stats_step(i, 2)
                ln2_moments_step(i, 2)
                ln2_var_step(i, 0)
                if not last:
                    split_xn(i, 0)
                    split_xn(i, 1)
                residual(i, 3)
                ln2_var_step(i, 1)
                ln2_normalise(i, 0)
                ln2_normalise(i, 1)
                y_step(f, 1, head=head)
                y_step(f, 2)
                split_x2n(i, 0, last)
                split_x2n(i, 1, last)
                y_step(f, 3)

            both(1, head=True)
            with dve.Fori(2, NS - 1) as i:
                both(i)
            both(NS - 1, last=True)
            f = NS - 1
            z_lo(f, LAST_Z)

            def last_relu(m):
                dve.wait_ge(h_filled, KH * f + m + 1)
                dve.tensor_scalar(relu[:, m % RING], LAST_H[m], scale1[:, m, 0:1], 0.0, ALU.mult,
                                  ALU.max).then_inc(dve_relu_done, 1)

            def last_square(m):
                wait_last_relu(dve, m)
                dve.tensor_tensor(square[:, m % RING], relu[:, m % RING], relu[:, m % RING],
                                  ALU.mult).then_inc(square_odd_done, 1)

            def last_split(m):
                dve.wait_ge(square_odd_done if m % 2 else square_even_done, m // 2 + 1)
                dve.wait_ge(r2_hi_done, KH * f + m + 1)
                dve.tensor_tensor(r2_lo[:, m], square[:, m % RING], r2_hi[:, m].bitcast(F32),
                                  ALU.subtract).then_inc(r2_lo_done, 1)

            last_relu(1)
            last_square(1)
            last_split(0)
            last_split(1)
            last_relu(4)
            last_square(3)
            last_split(2)
            last_split(3)
            last_square(5)
            last_split(4)
            last_split(5)
            last_square(7)
            last_split(6)
            last_split(7)
            for t in range(TT):
                if t == 0:
                    dve.wait_ge(y_added, TT * f)
                dve.wait_ge(y_filled, TT * f + t + 1)
                dve.tensor_tensor(y_scaled[:, t % 2], LAST_Y[t][:, 0:D], col_scale[:], ALU.mult).then_inc(y_scaled_done, 1)
                dve.wait_ge(y_scaled_done, TT * f + t + 1)
                dve.tensor_tensor(x_sb[:, f, t], y_scaled[:, t % 2], x_sb[:, f, t], ALU.add).then_inc(y_last_added, 1)

        @block.tensor
        def _(pe):
            pe.wait_ge(ident_ready, 1)
            for n in range(6):
                pe.transpose(banks[7][:, 0:P], ident[:], ident[:])
            pe.wait_ge(ctx_in, 16)
            for k in range(2):
                for b in range(B):
                    at = P * (B * k + b)
                    last = pe.transpose(banks[0][0:CH, at:at + J], ctx_sb[0:J, b, CH * k:CH * k + CH], ident[0:J, 0:J])
            last.then_inc(ctxT_filled, 1)

            def project_context(bank, w, c):
                for k in range(2):
                    last = pe.matmul(bank[:, 0:BJ], w[:, k, P * c:P * c + P], ctxT[:, k],
                                     start=(k == 0), stop=(k == 1))
                return last

            def transpose_ln(src, fill):
                for k in range(KD):
                    if fill(k) is not None:
                        pe.wait_ge(t_lo_done, fill(k) - 1)
                    for t in range(TT):
                        last = pe.transpose(ps_t[:, (1 + k) % 2, P * t:P * t + P], src[:, t, P * k:P * k + P], ident[:])
                    last.then_inc(t_filled, 1)

            def transpose_probs(i, c):
                if c < TT - 1:
                    pe.wait_ge(p_ready, (TT - 1) * i + c + 1)
                elif c == TT - 1:
                    pe.wait_ge(p_last_ready, i + 1)
                pe.wait_ge(t_lo_done, probs_fill(i, c) - {0: 0, 1: 2}.get(c, 1))
                for n in range(TT):
                    t, chunk = (c, n) if c < TT else (n, KC - 1)
                    rows = P if c < TT else LASTROWS
                    last = pe.transpose(ps_t[0:rows, c % 2, P * n:P * n + P], probs[:, t, P * chunk:P * chunk + rows],
                                        ident[:])
                last.then_inc(t_filled, 1)

            def scores(i, t, first=False, to=ps_s):
                if t == 0 and not first:
                    pe.wait_ge(x2_done, TT * i)
                    pe.wait_ge(y_scaled_done, TT * (i - 2) + 2)
                elif not first:
                    pe.wait_ge(shifted, TT * (i - 1) + t)
                for half in range(2):
                    cols = slice(HALF * half, HALF * half + HALF)
                    ps = to[:, half, 0:HALF]
                    pe.matmul(ps, ones_bf[:], mask_bias[:, batch(i), cols], start=True, stop=False)
                    for k in range(KD):
                        hi, lo = xnT_hi[:, k, P * t:P * t + P], xnT_lo[:, k, P * t:P * t + P]
                        pe.matmul(ps, hi, a_hi[:, k, batch(i), cols], start=False, stop=False)
                        pe.matmul(ps, hi, a_lo[:, k, batch(i), cols], start=False, stop=False)
                        last = pe.matmul(ps, lo, a_hi[:, k, batch(i), cols], start=False, stop=(k == KD - 1))
                last.then_inc(s_filled, 1)

            def attend(i, t, head=False, first=False):
                if first:
                    if t >= 2:
                        pe.wait_ge(x2_done, t - 1)
                elif t == 0:
                    pe.wait_ge(shifted, TT * i)
                elif t == 2 and head:
                    pe.wait_ge(w2T_ready, 2)
                elif t == 2:
                    pe.wait_ge(y_scaled_done, TT * (i - 1))
                elif t == 3:
                    pe.wait_ge(x2_done, TT * i + 1)
                ps = (FIRST_OUT if first else ATTN_OUT)[t][:, 0:D]
                pe.wait_ge(t_lo_done, probs_fill(i, t) + 1)
                for c in range(KC):
                    if t == 0 and c == KC - 1:
                        pe.wait_ge(t_lo_done, probs_fill(i, c) + 1)
                    rows = P if c < KC - 1 else LASTROWS
                    hi, lo = pT_hi[0:rows, c, P * t:P * t + P], pT_lo[0:rows, c, P * t:P * t + P]
                    at = batch(i) * KC + c
                    pe.matmul(ps, hi, vo_hi[0:rows, at], start=(c == 0), stop=False)
                    pe.matmul(ps, hi, vo_lo[0:rows, at], start=False, stop=False)
                    last = pe.matmul(ps, lo, vo_hi[0:rows, at], start=False, stop=(c == KC - 1))
                last.then_inc(o_filled, 1)

            def low_rank(f, to=ps_h[:, 1]):
                for k, hi in ((0, True), (0, False), (1, False), (1, True)):
                    if hi:
                        last = pe.matmul(to, bvT[:, k], x2nT_hi[:, k], start=(k == 0), stop=(k == 1))
                    else:
                        pe.matmul(to[0:3 * GP], bvT[:, k, 0:3 * GP], x2nT_lo[:, k], start=False, stop=False)
                last.then_inc(z_filled, 1)

            def hidden_main(f, m, to=None):
                ps = ps_h[:, m % 2] if to is None else to
                for k in range(KD):
                    pe.matmul(ps, w1T[:, k, m], x2nT_hi[:, k], start=(k == 0), stop=False)
                    pe.matmul(ps, w1T[:, k, m], x2nT_lo[:, k], start=False, stop=False)

            def hidden_low(m, to=None):
                pe.matmul(ps_h[:, m % 2] if to is None else to, uT[:, m], z[:], start=False, stop=True).then_inc(h_filled, 1)

            def hidden(f, m):
                if m == 1:
                    pe.wait_ge(z_ready, f + 1)
                else:
                    pe.wait_ge(relu_done, KH * f + m - 1)
                hidden_main(f, m)
                hidden_low(m)

            def project_out(f, t, head=False, tiles=range(KH)):
                if tiles[0] == 0:
                    if t == 0 and not head:
                        pe.wait_ge(y_scaled_done, TT * f - 1)
                    elif t == 2:
                        pe.wait_ge(y_scaled_done, TT * f + 1)
                    elif t != 0:
                        pe.wait_ge(x2_done, TT * (f + 1) + {1: 2, 3: 3}[t])
                ps = FFN_OUT[t][:, 0:D]
                for m in tiles:
                    if t == 0:
                        pe.wait_ge(r2_lo_done, KH * f + m + 1)
                    pe.matmul(ps, r2_hi[:, m, P * t:P * t + P], w2T[:, m], start=(m == 0), stop=False)
                    out_mm = pe.matmul(ps, r2_lo[:, m, P * t:P * t + P], w2T[:, m],
                                       start=False, stop=(m == KH - 1))
                if tiles[-1] == KH - 1:
                    out_mm.then_inc(y_filled, 1)

            def key_chunks(n):
                for c in range(2):
                    last = project_context(banks[5 + n][:, 256 * c:256 * c + 256], wk_sb, 2 * n + c)
                last.then_inc(k_filled, 1)

            for n in range(4):
                pe.transpose(banks[7][:, 0:P], ident[:], ident[:])
            pe.wait_ge(ctxT_ready, 1)
            pe.wait_ge(wk_in, 16)
            key_chunks(0)
            pe.wait_ge(wq_in, 16)
            for n in range(2):
                for c in range(2):
                    for k in range(KD):
                        cc = 2 * n + c
                        last = pe.transpose(banks[(1, 4)[n]][:, 256 * c + P * k:256 * c + P * k + P],
                                            wq_sb[:, k, P * cc:P * cc + P], ident[:])
                last.then_inc(wqT_filled, 1)
            key_chunks(1)
            pe.wait_ge(wqT_ready, 2)
            for n in range(KD * KI):
                c, m = divmod(n, KD)
                pe.wait_ge(k_ready, c // 2 + 1)
                if n == 4:
                    pe.wait_ge(k_ready, 2)
                if n >= 6:
                    pe.wait_ge(a_lo_done, n - 5)
                pe.matmul(banks[A_BANKS[n]][:, 0:2 * BJ], wqT[:, c, P * m:P * m + P], kT[:, 2 * c:2 * c + 2, :],
                          start=True, stop=True).then_inc(a_filled, 1)
            pe.wait_ge(xn_ready, 1)
            transpose_ln(xn, lambda k: None if k < 2 else k)
            pe.wait_ge(wv_in, 16)
            for n in range(2):
                pe.wait_ge(a_lo_done, 4 + n)
                for c in range(2):
                    last = project_context(banks[4 + n][:, 256 * c:256 * c + 256], wv_sb, 2 * n + c)
                last.then_inc(v_filled, 1)
            pe.wait_ge(a_lo_done, KD * KI)
            pe.wait_ge(t_lo_done, KD)
            pe.wait_ge(mask_ready, 1)
            scores(0, 0, first=True)

            def value_out(n):
                if n == 4:
                    pe.wait_ge(vo_lo_done, 3)
                for q in range(2):
                    b, tile = divmod(2 * n + q, KC)
                    ps = banks[VO_BANKS[n]][:, D * q:D * q + D]
                    terms = [(vT[:, b, c, P * (tile - c):P * (tile - c) + P], wo_sb[:, c]) for c in (tile - 1, tile)
                             if 0 <= c < KI]
                    if tile == 0:
                        terms.append((head0_rows[:], bo_row[:]))
                    for at, (lhsT, rhs) in enumerate(terms):
                        last = pe.matmul(ps, lhsT, rhs, start=(at == 0), stop=(at == len(terms) - 1))
                last.then_inc(vo_filled, 1)

            def scores0(t):
                if t >= 2:
                    pe.wait_ge(exp_done, t - 1)
                scores(0, t, first=True, to=SCORES0[t])

            pe.wait_ge(v_ready, 2)
            pe.wait_ge(wo_in, 16)
            pe.wait_ge(bo_in, 16)
            value_out(0)
            scores0(1)
            value_out(1)
            scores0(2)
            value_out(2)
            scores0(3)
            value_out(3)
            pe.wait_ge(select_ready, 1)
            pe.wait_ge(lowrank_in, 48)
            pe.wait_ge(diag2_ready, 1)
            pe.wait_ge(consts_ready, 9)
            pe.wait_ge(exp_done, 3)
            pe.matmul(banks[0][0:RANK, 0:P], fb_sb[:], select[:].rearrange("r g n -> r (g n)"), start=True, stop=True)
            for k in range(KD):
                last = pe.matmul(banks[0][:, P + P * k:P + P * k + P], ones[:], diag2[:, k], start=True, stop=True)
            last.then_inc(bank0_filled, 1)
            pe.wait_ge(vo_lo_done, 2)
            transpose_probs(0, 0)
            value_out(4)
            transpose_probs(0, 1)
            pe.wait_ge(fbT_ready, 1)
            for k in range(KD):
                last = pe.matmul(banks[1][:, P * k:P * k + P], v_sb[:, P * k:P * k + P], fbT[:], start=True, stop=True)
            last.then_inc(bvT_filled, 1)
            pe.wait_ge(ident_bf_ready, 1)
            pe.wait_ge(tern1_done, KH)
            pe.wait_ge(exp_done, 4)
            for k in range(KD):
                ps = ps_o[:, k].bitcast(BF16)
                for m in range(KH):
                    last = pe.transpose(ps[:, P * m:P * m + P], tern1[:, m, P * k:P * k + P], ident_bf[:])
                last.then_inc(w1T_filled, 1)

            def transpose_u(n):
                for q in range(4):
                    last = pe.transpose(banks[4 + n][:, P * q:P * q + P], u_groups[:, 4 * n + q], ident[:])
                last.then_inc(uT_filled, 1)

            pe.wait_ge(u_ready, 1)
            pe.wait_ge(vo_lo_done, 5)
            transpose_u(0)
            transpose_probs(0, 2)
            transpose_probs(0, 3)
            transpose_u(1)
            transpose_probs(0, 4)
            pe.wait_ge(w1T_ready, 1)
            attend(0, 0, first=True)
            pe.wait_ge(w1T_ready, 2)
            attend(0, 1, first=True)
            attend(0, 2, first=True)
            pe.wait_ge(xn_ready, 2)
            transpose_ln(xn, lambda k: ln1_fill(0, k))
            attend(0, 3, first=True)
            pe.wait_ge(col_ready, 1)
            pe.wait_ge(bvT_ready, 1)

            def transpose_w2():
                pe.wait_ge(tern2_pool_half_done, 1)
                pe.wait_ge(tern2_dve_half_done, 1)
                pe.wait_ge(x2_done, TT)
                t2 = tern2[:].rearrange("p k (q t) -> p k t q", t=KH)
                for n in range(2):
                    ps = ps_o[:, n].bitcast(BF16).rearrange("p (t d) -> p t d", t=4)
                    for q in range(4):
                        for k in range(KD):
                            last = pe.transpose(ps[:, q, P * k:P * k + P], t2[:, k, 4 * n + q], ident_bf[:])
                    last.then_inc(w2T_filled, 1)

            def both(i, last=False, head=False):
                f = i - 1
                pe.wait_ge(t_lo_done, ln1_fill(f, KD - 1) + 1)
                scores(i, 0, first=head)
                if head:
                    transpose_w2()
                    pe.wait_ge(x2n_ready, 2)
                    transpose_ln(x2n, lambda k: ln2_fill(0, k, False))
                    scores(i, 1)
                pe.wait_ge(t_lo_done, ln2_fill(f, KD - 1, False) + 1)
                if head:
                    pe.wait_ge(w2T_ready, 1)
                    low_rank(f, FIRST_Z)
                    pe.wait_ge(uT_ready, 2)
                    hidden_main(f, 0)
                    hidden_main(f, 1)
                    pe.wait_ge(z_ready, f + 1)
                    hidden_low(0)
                    hidden_low(1)
                else:
                    pe.wait_ge(relu_done, KH * f)
                    low_rank(f)
                    hidden_main(f, 0)
                    scores(i, 1)
                    pe.wait_ge(z_ready, f + 1)
                    hidden_low(0)
                    hidden(f, 1)
                    transpose_probs(i, 0)
                scores(i, 2)
                if head:
                    transpose_probs(i, 0)
                hidden(f, 2)
                hidden(f, 3)
                scores(i, 3)
                transpose_probs(i, 1)
                hidden(f, 4)
                hidden(f, 5)
                hidden(f, 6)
                transpose_probs(i, 2)
                hidden(f, 7)
                transpose_probs(i, 3)
                transpose_probs(i, 4)
                project_out(f, 0, head, tiles=range(0, 4))
                attend(i, 0, head)
                attend(i, 1)
                attend(i, 2)
                project_out(f, 0, tiles=range(4, KH))
                if not last:
                    pe.wait_ge(xn_ready, i + 2)
                    transpose_ln(xn, lambda k: ln1_fill(i, k))
                attend(i, 3)
                project_out(f, 1)
                project_out(f, 2)
                pe.wait_ge(x2n_ready, 2 * i + 2)
                transpose_ln(x2n, lambda k: ln2_fill(i, k, last))
                project_out(f, 3)

            both(1, head=True)
            with pe.Fori(2, NS - 1) as i:
                both(i)
            both(NS - 1, last=True)
            pe.wait_ge(t_lo_done, ln2_fill(NS - 1, KD - 1, True) + 1)
            f = NS - 1
            pe.wait_ge(y_scaled_done, TT * f - 2)
            low_rank(f, LAST_Z)
            pe.wait_ge(relu_done, KH * f)
            hidden_main(f, 0, LAST_H[0])
            hidden_main(f, 1, LAST_H[1])
            pe.wait_ge(z_ready, NS)
            hidden_low(0, LAST_H[0])
            hidden_low(1, LAST_H[1])
            for m in range(2, KH):
                if m >= 6:
                    wait_last_relu(pe, m - 6)
                hidden_main(f, m, LAST_H[m])
                hidden_low(m, LAST_H[m])

            def last_out(t, tiles):
                for m in tiles:
                    pe.wait_ge(r2_lo_done, KH * f + m + 1)
                    pe.matmul(LAST_Y[t][:, 0:D], r2_hi[:, m, P * t:P * t + P], w2T[:, m], start=(m == 0), stop=False)
                    last = pe.matmul(LAST_Y[t][:, 0:D], r2_lo[:, m, P * t:P * t + P], w2T[:, m],
                                     start=False, stop=(m == KH - 1))
                if tiles[-1] == KH - 1:
                    last.then_inc(y_filled, 1)

            pe.wait_ge(y_scaled_done, TT * f)
            for m in range(6):
                last_out(0, (m,))
                last_out(1, (m,))
            wait_last_relu(pe, 2)
            last_out(2, range(6))
            for t in range(3):
                last_out(t, range(6, KH))
            wait_last_relu(pe, 3)
            last_out(3, range(KH))


_INS = ['x', 'ctx_768', 'mask_BxS2_bk0', 'g_xattn', 'g_ffn', 'L0_xattn_W_q', 'L0_xattn_W_k', 'L0_xattn_W_v',
        'L0_xattn_W_o', 'L0_xattn_b_o', 'L0_ffn_fast_b', 'L0_ffn_w_fc', 'L0_ffn_w_proj', 'L0_ffn_u', 'L0_ffn_v',
        'L0_ffn_gate']


def kernel(**inputs):
    import numpy as _np
    import concourse.bacc as _bacc
    from concourse import mybir as _mybir
    from concourse.bass_utils import run_bass_kernel_spmd as _run

    nc = _bacc.Bacc("TRN2", target_bir_lowering=False, num_devices=1)
    arrays, args = {}, []
    for name in _INS:
        a = _np.ascontiguousarray(inputs[name])
        if a.ndim == 0:
            a = a.reshape(1)
        arrays[f"in_{name}_dram"] = a
        args.append(nc.dram_tensor(f"in_{name}_dram", a.shape, _mybir.dt.from_np(a.dtype), kind="ExternalInput").ap())
    shape = inputs['x'].shape
    args.append(nc.dram_tensor("out_0_dram", shape, _mybir.dt.float32, kind="ExternalOutput").ap())
    block_kernel(nc, *args)
    r = _run(nc, [arrays], core_ids=[0])
    return r.results[0]["out_0_dram"]
```
